# Optimizing a Trainium2 kernel written in Bass

```python
import numpy as np
import jax
import jax.numpy as jnp

def _softmax(x, axis=-1):
    return jax.nn.softmax(x, axis=axis)

def _gelu(x):
    return jax.nn.gelu(x, approximate=True)

def _silu(x):
    return jax.nn.silu(x)

def _sigmoid(x):
    return jax.nn.sigmoid(x)

def _layernorm(x, axis=-1, eps=1e-05):
    m = jnp.mean(x, axis=axis, keepdims=True)
    v = jnp.var(x, axis=axis, keepdims=True)
    return (x - m) / jnp.sqrt(v + eps)

def _scatter_add(tgt, idx, src, axis=0):
    return tgt.at[idx].add(src)

def _segment_sum(src, seg, n):
    return jax.ops.segment_sum(src, seg, n)
kernel_name = 'mk_decoder_preln_d1_seqx_r2_84d666'

def setup_inputs(seed: int=0):
    np.random.seed(seed)
    _w = jnp.asarray

    def _rec_inputs():
        import jax
        import jax.numpy as jnp
        _rk = jax.random.key(seed)
        x = -0.0002928 + 1 * jax.random.normal(jax.random.fold_in(_rk, 1), (16, 100, 512), jnp.float32)
        _lenS = 100 - jax.random.randint(jax.random.fold_in(_rk, 7), (16,), 0, max(1, 100 // 4) + 1, jnp.int32)
        _lenS2 = 722 - jax.random.randint(jax.random.fold_in(_rk, 8), (16,), 0, max(1, 722 // 4) + 1, jnp.int32)
        _ctx_1024P = jax.random.normal(jax.random.fold_in(_rk, 11), (16, 16, 512), jnp.float32)
        _ctx_1024c = jax.random.dirichlet(jax.random.fold_in(_rk, 511), 0.3 * jnp.ones((16,), jnp.float32), (16, 722))
        _ctx_1024t = jnp.einsum('bsk,bkd->bsd', _ctx_1024c, _ctx_1024P)
        _ctx_1024t = _ctx_1024t * jax.lax.rsqrt(jnp.mean(jnp.square(_ctx_1024t)) + 1e-12) * 0.953939
        ctx_1024 = 4.13588e-05 + 0.999923 * (_ctx_1024t + 0.3 * jax.random.normal(jax.random.fold_in(_rk, 611), (16, 722, 512), jnp.float32))
        return (x, ctx_1024)
    x, ctx_1024 = _rec_inputs()

    def _L0_attn_setup():
        import jax, jax.numpy as jnp
        import numpy as np
        D_MODEL = 512
        N_SH = 16
        N_BR = 4
        H_TOT = N_BR * N_SH
        DH = D_MODEL // N_SH
        BRANCH_CONFIGS = [(16, 0), (128, 16), (128, 0), (256, 144)]

        def rms_norm(x):
            eps = jnp.finfo(x.dtype).eps
            return x * jax.lax.rsqrt(jnp.mean(x * x, axis=-1, keepdims=True) + eps)

        def rope(x):
            T, Dh = (x.shape[2], x.shape[3])
            inv_freq = 1.0 / 10000.0 ** (jnp.arange(0, Dh, 2, dtype=jnp.float32) / Dh)
            freqs = jnp.arange(T, dtype=jnp.float32)[:, None] * inv_freq[None, :]
            cos = jnp.cos(freqs)[None, None]
            sin = jnp.sin(freqs)[None, None]
            x1 = x[..., 0::2]
            x2 = x[..., 1::2]
            return jnp.concatenate([-x2 * sin + x1 * cos, x1 * sin + x2 * cos], axis=-1)
        key = jax.random.key(seed)
        ks = jax.random.split(key, 12)
        B, T, C = (2, 512, D_MODEL)
        s = 0.02
        return {'X': jax.random.normal(ks[0], (B, T, C), jnp.float32), 'WQ': jax.random.normal(ks[1], (C, H_TOT * DH), jnp.float32) * s, 'bQ': jax.random.normal(ks[2], (H_TOT * DH,), jnp.float32) * s, 'WK': jax.random.normal(ks[3], (C, C), jnp.float32) * s, 'bK': jax.random.normal(ks[4], (C,), jnp.float32) * s, 'WV': jax.random.normal(ks[5], (C, H_TOT * DH), jnp.float32) * s, 'bV': jax.random.normal(ks[6], (H_TOT * DH,), jnp.float32) * s, 'WO': jax.random.normal(ks[7], (C, C), jnp.float32) * s, 'bO': jax.random.normal(ks[8], (C,), jnp.float32) * s, 'sink_scalars': jax.random.normal(ks[9], (H_TOT,), jnp.float32) * s, 'v_nulls': jax.random.normal(ks[10], (H_TOT, DH), jnp.float32) * s}
    _L0_attn_all = _L0_attn_setup()
    _L0_attn_in = {k: v for k, v in _L0_attn_all.items() if k in ('WQ', 'bQ', 'WK', 'bK', 'WV', 'bV', 'WO', 'bO', 'sink_scalars', 'v_nulls')}
    del _L0_attn_all

    def _L0_xattn_setup():
        import jax, jax.numpy as jnp
        import numpy as np
        HID, NH, TOPK = (512, 16, 32)
        HD = HID // NH
        SCALE = float(np.sqrt(HD))

        def _split_heads(x, B, L):
            return x.reshape(B, L, NH, HD).transpose(0, 2, 1, 3)
        key = jax.random.key(seed)
        ks = jax.random.split(key, 12)
        B, Q, KV = (2, 1024, 2048)
        s = 0.02
        return {'query': jax.random.normal(ks[0], (B, Q, HID), jnp.float32), 'key': jax.random.normal(ks[1], (B, KV, HID), jnp.float32), 'value': jax.random.normal(ks[2], (B, KV, HID), jnp.float32), 'Wq': jax.random.normal(ks[3], (HID, HID), jnp.float32) * s, 'bq': jnp.zeros((HID,), jnp.float32), 'Wk': jax.random.normal(ks[4], (HID, HID), jnp.float32) * s, 'bk': jnp.zeros((HID,), jnp.float32), 'Wv': jax.random.normal(ks[5], (HID, HID), jnp.float32) * s, 'bv': jnp.zeros((HID,), jnp.float32), 'Wo': jax.random.normal(ks[6], (HID, HID), jnp.float32) * s, 'bo': jnp.zeros((HID,), jnp.float32)}
    _L0_xattn_all = _L0_xattn_setup()
    _L0_xattn_in = {k: v for k, v in _L0_xattn_all.items() if k in ('Wq', 'bq', 'Wk', 'bk', 'Wv', 'bv', 'Wo', 'bo')}
    del _L0_xattn_all

    def _L0_ffn_setup():
        import jax, jax.numpy as jnp
        import numpy as np
        B, N, D = (4, 1024, 512)
        SPARSITY = 0.01
        key = jax.random.key(seed)
        k1, k2, k3 = jax.random.split(key, 3)
        x = jax.random.normal(k1, (B, N, D), dtype=jnp.float32)
        spatial = jax.random.normal(k2, (D, D), dtype=jnp.float32) * 0.02
        freq = jnp.fft.fft(spatial, axis=-1)
        k = int(D * SPARSITY)
        mag = jnp.abs(freq)
        kth = jax.lax.top_k(mag, k)[0][:, -1:]
        w_sparse = jnp.where(mag >= kth, freq, 0.0 + 0j)
        bias = jax.random.normal(k3, (D,), dtype=jnp.float32) * 0.01
        return {'x': x, 'w_freq_real': jnp.real(w_sparse).astype(jnp.float32), 'w_freq_imag': jnp.imag(w_sparse).astype(jnp.float32), 'bias': bias}
    _L0_ffn_all = _L0_ffn_setup()
    _L0_ffn_in = {k: v for k, v in _L0_ffn_all.items() if k in ('w_freq_real', 'w_freq_imag', 'bias')}
    del _L0_ffn_all
    return {'x': x, 'ctx_1024': ctx_1024, 'L0_attn_WQ': _L0_attn_in['WQ'], 'L0_attn_bQ': _L0_attn_in['bQ'], 'L0_attn_WK': _L0_attn_in['WK'], 'L0_attn_bK': _L0_attn_in['bK'], 'L0_attn_WV': _L0_attn_in['WV'], 'L0_attn_bV': _L0_attn_in['bV'], 'L0_attn_WO': _L0_attn_in['WO'], 'L0_attn_bO': _L0_attn_in['bO'], 'L0_attn_sink_scalars': _L0_attn_in['sink_scalars'], 'L0_attn_v_nulls': _L0_attn_in['v_nulls'], 'L0_xattn_Wq': _L0_xattn_in['Wq'], 'L0_xattn_bq': _L0_xattn_in['bq'], 'L0_xattn_Wk': _L0_xattn_in['Wk'], 'L0_xattn_bk': _L0_xattn_in['bk'], 'L0_xattn_Wv': _L0_xattn_in['Wv'], 'L0_xattn_bv': _L0_xattn_in['bv'], 'L0_xattn_Wo': _L0_xattn_in['Wo'], 'L0_xattn_bo': _L0_xattn_in['bo'], 'L0_ffn_w_freq_real': _L0_ffn_in['w_freq_real'], 'L0_ffn_w_freq_imag': _L0_ffn_in['w_freq_imag'], 'L0_ffn_bias': _L0_ffn_in['bias']}

def reference(x, ctx_1024, L0_attn_WQ, L0_attn_bQ, L0_attn_WK, L0_attn_bK, L0_attn_WV, L0_attn_bV, L0_attn_WO, L0_attn_bO, L0_attn_sink_scalars, L0_attn_v_nulls, L0_xattn_Wq, L0_xattn_bq, L0_xattn_Wk, L0_xattn_bk, L0_xattn_Wv, L0_xattn_bv, L0_xattn_Wo, L0_xattn_bo, L0_ffn_w_freq_real, L0_ffn_w_freq_imag, L0_ffn_bias):
    import jax
    import jax.numpy as jnp

    def _L0_attn_ref(X, WQ, bQ, WK, bK, WV, bV, WO, bO, sink_scalars, v_nulls):
        import jax, jax.numpy as jnp
        import numpy as np
        D_MODEL = 512
        N_SH = 16
        N_BR = 4
        H_TOT = N_BR * N_SH
        DH = D_MODEL // N_SH
        BRANCH_CONFIGS = [(16, 0), (128, 16), (128, 0), (256, 144)]

        def rms_norm(x):
            eps = jnp.finfo(x.dtype).eps
            return x * jax.lax.rsqrt(jnp.mean(x * x, axis=-1, keepdims=True) + eps)

        def rope(x):
            T, Dh = (x.shape[2], x.shape[3])
            inv_freq = 1.0 / 10000.0 ** (jnp.arange(0, Dh, 2, dtype=jnp.float32) / Dh)
            freqs = jnp.arange(T, dtype=jnp.float32)[:, None] * inv_freq[None, :]
            cos = jnp.cos(freqs)[None, None]
            sin = jnp.sin(freqs)[None, None]
            x1 = x[..., 0::2]
            x2 = x[..., 1::2]
            return jnp.concatenate([-x2 * sin + x1 * cos, x1 * sin + x2 * cos], axis=-1)
        B, T, C = X.shape
        q = (X @ WQ + bQ).reshape(B, T, H_TOT, DH).transpose(0, 2, 1, 3)
        q = rope(rms_norm(q))
        v = (X @ WV + bV).reshape(B, T, H_TOT, DH).transpose(0, 2, 1, 3)
        k = rope((X @ WK + bK).reshape(B, T, N_SH, DH).transpose(0, 2, 1, 3))
        k = jnp.tile(k, (1, N_BR, 1, 1))
        scores = jnp.einsum('bhqd,bhkd->bhqk', q, k)
        denom = jnp.sqrt(jnp.sum(k * k, axis=-1))[:, :, None, :]
        w = scores / denom
        idx = jnp.arange(T)
        dist = idx[:, None] - idx[None, :]
        bmasks = jnp.stack([((dist >= g) & (dist < h)).astype(w.dtype) for h, g in BRANCH_CONFIGS], axis=0)
        full_mask = jnp.repeat(bmasks, N_SH, axis=0)[None]
        w = w * full_mask
        sinks = jnp.broadcast_to(jnp.tanh(sink_scalars).reshape(1, H_TOT, 1, 1), (B, H_TOT, T, 1))
        probs = jax.nn.softmax(jnp.concatenate([w, sinks], axis=-1), axis=-1)
        out = jnp.einsum('bhqk,bhkd->bhqd', probs[..., :T], v)
        out = out + probs[..., T:] * v_nulls.reshape(1, H_TOT, 1, DH)
        ctx = out.reshape(B, N_BR, N_SH, T, DH).transpose(0, 1, 3, 2, 4).reshape(B, N_BR, T, C)
        y = ctx @ WO + bO
        return y.mean(axis=1)

    def _L0_xattn_ref(query, key, value, Wq, bq, Wk, bk, Wv, bv, Wo, bo):
        import jax, jax.numpy as jnp
        import numpy as np
        HID, NH, TOPK = (512, 16, 32)
        HD = HID // NH
        SCALE = float(np.sqrt(HD))

        def _split_heads(x, B, L):
            return x.reshape(B, L, NH, HD).transpose(0, 2, 1, 3)
        B, Q, _ = query.shape
        KV = key.shape[1]
        q = _split_heads(query @ Wq.T + bq, B, Q)
        k = _split_heads(key @ Wk.T + bk, B, KV)
        v = _split_heads(value @ Wv.T + bv, B, KV)
        scores = jnp.einsum('bhqd,bhkd->bhqk', q, k) / SCALE
        eff_k = min(TOPK, KV)
        top_scores, top_idx = jax.lax.top_k(scores, eff_k)
        w = jax.nn.softmax(top_scores, axis=-1)
        top_v = jnp.take_along_axis(v[:, :, None, :, :], top_idx[..., None], axis=3)
        out = jnp.einsum('bhqk,bhqkd->bhqd', w, top_v)
        out = out.transpose(0, 2, 1, 3).reshape(B, Q, HID)
        return out @ Wo.T + bo

    def _L0_ffn_ref(x, w_freq_real, w_freq_imag, bias):
        import jax, jax.numpy as jnp
        import numpy as np
        B, N, D = (4, 1024, 512)
        SPARSITY = 0.01
        w = jax.lax.complex(w_freq_real, w_freq_imag)
        x_freq = jnp.fft.fft(x, axis=-1)
        y_freq = jnp.einsum('bnd,do->bno', x_freq, w)
        y = jnp.real(jnp.fft.ifft(y_freq, axis=-1))
        return y + bias
    x = x + _L0_attn_ref(_layernorm(x, axis=-1), L0_attn_WQ, L0_attn_bQ, L0_attn_WK, L0_attn_bK, L0_attn_WV, L0_attn_bV, L0_attn_WO, L0_attn_bO, L0_attn_sink_scalars, L0_attn_v_nulls)
    x = x + _L0_xattn_ref(_layernorm(x, axis=-1), ctx_1024, ctx_1024, L0_xattn_Wq, L0_xattn_bq, L0_xattn_Wk, L0_xattn_bk, L0_xattn_Wv, L0_xattn_bv, L0_xattn_Wo, L0_xattn_bo)
    x = x + _L0_ffn_ref(_layernorm(x, axis=-1), L0_ffn_w_freq_real, L0_ffn_w_freq_imag, L0_ffn_bias)
    return x

_drawn_inputs = setup_inputs


def setup_inputs(seed=0):
    import zlib

    import numpy as np

    out = dict(_drawn_inputs(seed))
    spreads = {'L0_xattn_bq': (0.0, 0.1),
     'L0_xattn_bk': (0.0, 2.0),
     'L0_xattn_bv': (0.0, 0.1),
     'L0_xattn_bo': (0.0, 0.1)}
    factors = {'L0_attn_WQ': 7.073,
     'L0_attn_bQ': 54.015,
     'L0_attn_WK': 7.092,
     'L0_attn_bK': 64.0,
     'L0_attn_WV': 4.288,
     'L0_attn_bV': 8.0,
     'L0_attn_WO': 4.112,
     'L0_attn_bO': 2.677,
     'L0_attn_sink_scalars': 200.0,
     'L0_attn_v_nulls': 200.0,
     'L0_ffn_bias': 8.0}
    for name, (base, spread) in spreads.items():
        noise = np.random.default_rng([zlib.crc32(name.encode()), seed]).standard_normal(out[name].shape)
        drawn = base * np.exp(spread * noise) if base else spread * noise
        out[name] = jnp.asarray(drawn.astype(out[name].dtype))
    for name, factor in factors.items():
        out[name] = (out[name] * factor).astype(out[name].dtype)
    return out
```

```python
from contextlib import ExitStack

import numpy as np
import concourse.bass as bass
import concourse.mybir as mybir

F32 = mybir.dt.float32
F32R = mybir.dt.float32r
ALU = mybir.AluOpType
ACT = mybir.ActivationFunctionType
AX = mybir.AxisListType

B, T, D, KV = 16, 100, 512, 722
DH, NH, NBR = 32, 16, 4
CC = D // 128
BRANCHES = [(16, 0), (128, 16), (128, 0), (256, 144)]
LIVE = [br for br, (high, low) in enumerate(BRANCHES) if low < T]
NL = len(LIVE)
assert LIVE == list(range(NL)) and NL == NBR - 1
TOPK = 32
SCALE = DH ** -0.5
LN_EPS = 1e-5
RMS_EPS = float(np.finfo(np.float32).eps)
REMOVED = -3.0e38


class At:

    def __init__(self, const, reg=None, factor=1):
        self.const, self.reg, self.factor = const, reg, factor

    def next(self, n=1):
        return At(self.const + n, self.reg, self.factor)

    def count(self, per, k):
        n = self.const * per + k
        return n if self.reg is None else self.reg * (self.factor * per) + n


def need(eng, sem, value):
    if not isinstance(value, int) or value > 0:
        eng.wait_ge(sem, value)


def settle(eng):
    eng.nop(nofuse=True)


class Order:

    def __init__(self, eng, sem):
        self.eng, self.sem, self.n = eng, sem, 0

    def mark(self, ins):
        ins.then_inc(self.sem, 1)
        self.n += 1
        return self.n

    def after(self, n):
        self.eng.wait_ge(self.sem, n)

    def finish(self):
        if self.n:
            self.eng.wait_ge(self.sem, self.n)
            self.eng.sem_clear(self.sem)
        self.n = 0


def split3(pe, out, ah, al, bh, bl, start, stop):
    pe.matmul(out, ah, bh, start=start, stop=False)
    pe.matmul(out, ah, bl, start=False, stop=False)
    return pe.matmul(out, al, bh, start=False, stop=stop)


def row_stats(dve, order, x, stats, mv, done):
    order.after(order.mark(dve.bn_stats(stats, x)))
    order.after(order.mark(dve.bn_aggr(mv, stats)))
    dve.tensor_scalar(mv[:, 1:2], mv[:, 1:2], LN_EPS, None, ALU.add).then_inc(done, 1)


def spectral_program(nc, A, M):
    with ExitStack() as ctx:
        sb = lambda n, s, d=F32: ctx.enter_context(nc.sbuf_tensor(n, s, d))
        sem = lambda n: ctx.enter_context(nc.semaphore(n))
        mats = {n: sb("sp_" + n, [128, CC, D]) for n in ("wrT", "wiT", "dft_cos", "dft_sin", "dft_msin")}
        Br = sb("sp_Br", [128, CC, D])
        Bi = sb("sp_Bi", [128, CC, D])
        acc = ctx.enter_context(nc.psum_tensor("sp_acc", [128, 2, 512], F32))
        loaded = sem("sp_loaded")
        product = sem("sp_product")
        kept = sem("sp_kept")
        terms = [(Br, (("wrT", "dft_cos"), ("wiT", "dft_msin"))), (Bi, (("wrT", "dft_sin"), ("wiT", "dft_cos")))]
        block = ctx.enter_context(nc.Block())

        @block.sync
        def _(sp):
            for n, t in mats.items():
                sp.dma_start(t[:, :, :], A[n].rearrange("(c p) o -> p c o", p=128)).then_inc(loaded, 16)

        @block.tensor
        def _(pe):
            pe.wait_ge(loaded, 16 * len(mats))
            n = 0
            for _, pairs in terms:
                for kt in range(CC):
                    if n >= 2:
                        pe.wait_ge(kept, n - 1)
                    steps = [(l, r, c) for l, r in pairs for c in range(CC)]
                    for i, (l, r, c) in enumerate(steps):
                        last = pe.matmul(acc[:, n % 2, :], mats[l][:, c, 128 * kt:128 * kt + 128],
                                         mats[r][:, c, :], start=i == 0, stop=i == len(steps) - 1)
                    last.then_inc(product, 1)
                    n += 1
            pe.wait_ge(kept, n)
            for jt in range(CC):
                if jt >= 2:
                    pe.wait_ge(kept, n - 1)
                steps = [(l, r, c) for l, r in (("dft_cos", Br), ("dft_sin", Bi)) for c in range(CC)]
                for i, (l, r, c) in enumerate(steps):
                    last = pe.matmul(acc[:, n % 2, :], mats[l][:, c, 128 * jt:128 * jt + 128],
                                     r[:, c, :], start=i == 0, stop=i == len(steps) - 1)
                last.then_inc(product, 1)
                n += 1

        @block.scalar
        def _(act):
            outs = [(t[:, kt, :], 1.0) for t, _ in terms for kt in range(CC)]
            outs += [(M[:, jt, :], 1.0 / D) for jt in range(CC)]
            for n, (out, scale) in enumerate(outs):
                act.wait_ge(product, n + 1)
                act.activation(out, acc[:, n % 2, :], ACT.Copy, scale=scale).then_inc(kept, 1)


def self_program(nc, A, x1_dram):
    NQ = NL * D
    NQK = NQ + D
    QB = NQK // D
    HEADS = NQK // DH
    QC = NQK // 128
    HK = 4
    PV = HK * NL * (DH + 1)
    RING = 4
    with ExitStack() as ctx:
        sb = lambda n, s, d=F32: ctx.enter_context(nc.sbuf_tensor("sa_" + n, s, d))
        ps = lambda n, s: ctx.enter_context(nc.psum_tensor("sa_" + n, s, F32))
        sem = lambda n: ctx.enter_context(nc.semaphore("sa_" + n))
        heads = lambda t, n: t.rearrange("p (h d) -> p h d", h=n)
        WqkH, WqkL = sb("WqkH", [128, CC, NQK], F32R), sb("WqkL", [128, CC, NQK], F32R)
        Wv, WO = sb("Wv", [128, CC, NBR * D]), sb("WO", [128, CC, D])
        stage = sb("stage", [128, RING, D])
        ident = sb("ident", [128, 128])
        cos, sin = sb("cos", [T, DH // 2]), sb("sin", [T, DH // 2])
        bias_qk, bias_o = sb("bias_qk", [T, NQK]), sb("bias_o", [T, D])
        bv3, vn3, es3, k3, r3, cb = (sb(n, [128, CC]) for n in ("bv3", "vn3", "es3", "k3", "r3", "cb"))
        bvl = sb("bvl", [128, NL, CC])
        xin, xn, xres, x1 = (sb(n, [T, D]) for n in ("xin", "xn", "xres", "x1"))
        stats, mv, rstd = sb("stats", [T, 6]), sb("mv", [T, 2]), sb("rstd", [T, 1])
        xT = sb("xT", [128, CC, T])
        xTh, xTl = sb("xTh", [128, CC, T], F32R), sb("xTl", [128, CC, T], F32R)
        xsum, out3 = sb("xsum", [128, CC]), sb("out3", [128, CC])
        qk, rq, ss = sb("qk", [T, NQK]), sb("rq", [T, NQK]), sb("ss", [T, HEADS])
        minus_half, step = sb("minus_half", [T, HEADS]), sb("step", [1, 1])
        tmp = sb("tmp", [T, NQ])
        qkTh, qkTl = sb("qkTh", [128, QC, T], F32R), sb("qkTl", [128, QC, T], F32R)
        E = sb("E", [T + 1, NH, NL, T])
        V = sb("V", [T + 1, NH, NL, DH + 1])
        rden = sb("rden", [T, NH * NL])
        ctxr, ctxT = sb("ctxr", [T, D]), sb("ctxT", [128, CC, T])
        pp, pq = ps("pp", [128, 2, 512]), ps("pq", [128, 4, 512])
        pt, pw = ps("pt", [128, 512]), ps("pw", [128, 512])

        x_in, xres_in, x1_out = sem("x_in"), sem("xres_in"), sem("x1_out")
        setup_in, null_in = sem("setup_in"), sem("null_in")
        dve_order, pool_order = sem("dve_order"), sem("pool_order")
        staged = [sem(f"staged{r}") for r in range(RING)]
        hi_made, lo_made = sem("hi_made"), sem("lo_made")
        sink_steps, null_weights, null_values = sem("sink_steps"), sem("null_weights"), sem("null_values")
        xn_ready, xres_ready = sem("xn_ready"), sem("xres_ready")
        var_ready, rstd_ready, ss_ready, norm_ready = (sem(n) for n in ("var_ready", "rstd_ready", "ss_ready", "norm_ready"))
        xT_mm, xT_hi, xT_copy, xT_lo, sum_ready = (sem(n) for n in ("xT_mm", "xT_hi", "xT_copy", "xT_lo", "sum_ready"))
        v3_mm, out3_ready = sem("v3_mm"), sem("out3_ready")
        qk_mm, qk_ready, sq_ready, roped = sem("qk_mm"), sem("qk_ready"), sem("sq_ready"), sem("roped")
        v_mm, v_ready = sem("v_mm"), sem("v_ready")
        hT_mm, hT_hi, hT_lo = sem("hT_mm"), sem("hT_hi"), sem("hT_lo")
        s_mm, e_ready, masked = sem("s_mm"), sem("e_ready"), sem("masked")
        pv_mm, pv_used, ctx_ready = sem("pv_mm"), sem("pv_used"), sem("ctx_ready")
        cT_mm, cT_ready, y_mm, x1_ready = sem("cT_mm"), sem("cT_ready"), sem("y_mm"), sem("x1_ready")

        UNITS = [(c, n) for c in range(CC) for n in range(QB)]
        sinks0, tanh0, exp0 = (qk[0:1, 64 * n:64 * n + NH * NL] for n in range(3))
        SETUP = [
            (WO[:, :, :], A["WO"].rearrange("(c p) o -> p c o", p=128)),
            (ident[:, :], A["ident"]), (cos[:, :], A["cos"]), (sin[:, :], A["sin"]),
            (bias_qk[:, 0:NQ], A["bQ"][0:1, 0:NQ].broadcast_to((T, NQ))),
            (bias_qk[:, NQ:NQK], A["bK"][0:1, :].broadcast_to((T, D))),
            (bias_o[:, :], A["bO"][0:1, :].broadcast_to((T, D))),
            (bv3[:, :], A["bV_cols"][:, NL * CC:]),
            (vn3[:, :], A["v_nulls_cols"][:, NL * CC:]),
            (es3[:, :], A["sinks_cols"][:, NL * CC:]),
            (sinks0, A["sinks"][0:1, 0:NL * NH]),
            (rq[0:1, 0:NQ], A["v_nulls"][0:1, 0:NQ]),
            (tmp[0:1, 0:NQ], A["bV"][0:1, 0:NQ]),
        ]
        SETUP += [(bvl[:, n, :], A["bV_cols"][:, CC * n:CC * n + CC]) for n in range(NL)]
        SETUP += [(Wv[:, c, :], A["WV"][128 * c:128 * c + 128, :]) for c in range(CC)]

        block = ctx.enter_context(nc.Block())

        def each_batch(eng, body):
            body(At(-1), cur=False, prev=False, nxt=True)
            body(At(0), cur=True, prev=False, nxt=True)
            with eng.Fori(1, B - 1) as i:
                body(At(0, i), cur=True, prev=True, nxt=True)
            body(At(B - 1), cur=True, prev=True, nxt=False)
            body(At(B), cur=False, prev=True, nxt=False)

        def batch_of(dram, b, n):
            i = b.const + n if b.reg is None else b.reg + (b.const + n)
            return dram[bass.ds(i, 1)].rearrange("o t d -> (o t) d")

        @block.sync
        def _(sp):
            for u, (c, n) in enumerate(UNITS):
                if u >= RING:
                    sp.wait_ge(hi_made, u - RING + 1)
                    sp.wait_ge(lo_made, u - RING + 1)
                rows = slice(128 * c, 128 * c + 128)
                src = A["WQ"][rows, D * n:D * n + D] if n < NL else A["WK"][rows, :]
                sp.dma_start(stage[:, u % RING, :], src).then_inc(staged[u % RING], 16)

            def body(b, cur, prev, nxt):
                if nxt:
                    need(sp, xn_ready, b.count(1, 1))
                    sp.dma_start(xin[:, :], batch_of(A["x"], b, 1)).then_inc(x_in, 16)
                if prev:
                    need(sp, x1_ready, b.count(1, -1))
                    sp.dma_start(xres[:, :], batch_of(A["x"], b, -1)).then_inc(xres_in, 16)
                    sp.wait_ge(x1_ready, b.count(1, 0))
                    sp.dma_start(batch_of(x1_dram, b, -1), x1[:, :]).then_inc(x1_out, 16)
            each_batch(sp, body)
            sp.wait_ge(x1_out, 16 * B)

        @block.gpsimd
        def _(pool):
            for t, a in SETUP:
                pool.dma_start(t, a).then_inc(setup_in, 16)
            pool.wait_ge(null_weights, 1)
            pool.dma_start(E[T:T + 1, :, :, :].rearrange("p h n q -> p (h n q)"),
                           E[0:1, :, :, :].rearrange("p h n q -> p (h n q)")).then_inc(null_in, 16)
            pool.wait_ge(null_values, 1)
            pool.dma_start(V[T:T + 1, :, :, :].rearrange("p h n d -> p (h n d)"),
                           V[0:1, :, :, :].rearrange("p h n d -> p (h n d)")).then_inc(null_in, 16)
            order = Order(pool, pool_order)
            order.mark(pool.memset(minus_half[:, :], -0.5))
            order.finish()
            one = pool.to_reg(1.0)

            def body(b, cur, prev, nxt):
                if cur:
                    pool.wait_ge(ss_ready, b.count(1, 1))
                    pool.tensor_tensor(ss[:, :], ss[:, :], minus_half[:, :], ALU.pow).then_inc(norm_ready, 1)
                if prev:
                    pool.wait_ge(xres_in, b.count(16, 0))
                    pool.tensor_tensor(xres[:, :], xres[:, :], bias_o[:, :], ALU.add).then_inc(xres_ready, 1)
                if cur:
                    for g in range(NH // 4):
                        pool.wait_ge(e_ready, b.count(NH, 4 * g + 4))
                        order.mark(pool.tensor_tensor(step[:, :], minus_half[0:1, 0:1], minus_half[0:1, 0:1], ALU.mult))
                        for br in LIVE:
                            high, low = BRANCHES[br]
                            part = E[0:T, 4 * g:4 * g + 4, br, :]
                            windows = [(-low, 1)] + ([(high - 1, -1)] if high < T else [])
                            for base, sign in windows:
                                order.after(order.n)
                                ins = pool.affine_select(
                                    out=part, in_=part, compare_op=ALU.is_ge, fill=one, base=base,
                                    pattern=[[0, 4], [sign, T]], channel_multiplier=-sign)
                                if (g, br, sign) == (NH // 4 - 1, LIVE[-1], windows[-1][1]):
                                    ins.then_inc(masked, 1)
                                else:
                                    order.mark(ins)
                if nxt:
                    pool.wait_ge(var_ready, b.count(1, 2))
                    pool.tensor_tensor(rstd[:, :], mv[:, 1:2], minus_half[:, 0:1], ALU.pow).then_inc(rstd_ready, 1)
                order.finish()
            each_batch(pool, body)

        @block.scalar
        def _(act):
            for u, (c, n) in enumerate(UNITS):
                act.wait_ge(staged[u % RING], 16 * (u // RING + 1))
                act.activation(WqkH[:, c, D * n:D * n + D], stage[:, u % RING, :], ACT.Copy).then_inc(hi_made, 1)
            act.wait_ge(setup_in, 16 * len(SETUP))
            act.activation(tanh0, sinks0, ACT.Tanh).then_inc(sink_steps, 1)
            act.activation(r3[:, :], es3[:, :], ACT.Tanh).then_inc(sink_steps, 1)
            act.wait_ge(sink_steps, 2)
            act.activation(exp0, tanh0, ACT.Exp).then_inc(sink_steps, 1)
            act.activation(es3[:, :], r3[:, :], ACT.Exp).then_inc(sink_steps, 1)
            act.wait_ge(sink_steps, 4)
            for br in range(NL):
                w = exp0[:, NH * br:NH * br + NH].unsqueeze(2).broadcast_to((1, NH, T))
                last = act.activation(E[0:1, :, br, :], w, ACT.Copy)
            last.then_inc(null_weights, 1)

            def body(b, cur, prev, nxt):
                if cur:
                    act.wait_ge(xT_mm, b.count(1, 1))
                    act.activation(xTh[:, :, :], heads(pt[:, 0:CC * T], CC), ACT.Copy).then_inc(xT_hi, 1)
                    for n in range(QB):
                        if n == 0:
                            need(act, hT_mm, b.count(QC // 4, 0))
                        act.wait_ge(qk_ready, b.count(QB, n + 1))
                        act.activation(rq[:, D * n:D * n + D], qk[:, D * n:D * n + D], ACT.Square).then_inc(sq_ready, 1)
                    need(act, pv_mm, b.count(1, 0))
                    for br in range(NL):
                        act.wait_ge(v_mm, b.count(NL, br + 1))
                        act.activation(V[0:T, :, br, 0:DH], heads(pp[0:T, (QB + br) % 2, :], NH),
                                       ACT.Copy).then_inc(v_ready, 1)
                    for g in range(QC // 4):
                        act.wait_ge(hT_mm, b.count(QC // 4, g + 1))
                        act.activation(qkTh[:, 4 * g:4 * g + 4, :], heads(pp[:, (QB + NL + g) % 2, 0:4 * T], 4),
                                       ACT.Copy).then_inc(hT_hi, 1)
                    for h in range(NH):
                        act.wait_ge(s_mm, b.count(NH, h + 1))
                        act.activation(E[0:T, h, :, :], heads(pq[0:T, h % 4, 0:NL * T], NL), ACT.Exp).then_inc(e_ready, 1)
            each_batch(act, body)

        @block.vector
        def _(dve):
            for u, (c, n) in enumerate(UNITS):
                dve.wait_ge(hi_made, u + 1)
                dve.tensor_tensor(WqkL[:, c, D * n:D * n + D], stage[:, u % RING, :],
                                  WqkH[:, c, D * n:D * n + D].bitcast(F32), ALU.subtract).then_inc(lo_made, 1)
            order = Order(dve, dve_order)
            then = lambda ins: order.after(order.mark(ins))
            dve.wait_ge(setup_in, 16 * len(SETUP))
            then(dve.memset(V[:, :, :, :], 1.0))
            for br in range(NL):
                last = dve.tensor_tensor(V[0:1, :, br, 0:DH], heads(rq[0:1, D * br:D * br + D], NH),
                                         heads(tmp[0:1, D * br:D * br + D], NH), ALU.subtract)
                if br < NL - 1:
                    order.mark(last)
            order.after(order.n)
            last.then_inc(null_values, 1)
            then(dve.tensor_tensor(cb[:, :], bvl[:, 0, :], bvl[:, 1, :], ALU.add))
            then(dve.tensor_tensor(cb[:, :], cb[:, :], bvl[:, 2, :], ALU.add))
            then(dve.tensor_scalar(cb[:, :], cb[:, :], 1.0 / NBR, None, ALU.mult))
            dve.wait_ge(sink_steps, 4)
            then(dve.tensor_tensor(k3[:, :], es3[:, :], vn3[:, :], ALU.mult))
            then(dve.scalar_tensor_tensor(k3[:, :], bv3[:, :], float(T), k3[:, :], ALU.mult, ALU.add))
            then(dve.tensor_scalar(r3[:, :], es3[:, :], float(T), float(NBR), ALU.add, ALU.mult))
            then(dve.reciprocal(r3[:, :], r3[:, :]))
            dve.wait_ge(null_in, 32)
            order.finish()

            half = DH // 2
            qk3, rq3 = heads(qk[:, :], HEADS), heads(rq[:, :], HEADS)
            even, odd = qk3[:, :, 0:DH:2], qk3[:, :, 1:DH:2]
            first, second = rq3[:, :, 0:half], rq3[:, :, half:DH]
            t3 = heads(tmp[:, 0:HEADS * half], HEADS)
            cos3, sin3 = (t[:, :].unsqueeze(1).broadcast_to((T, HEADS, DH // 2)) for t in (cos, sin))
            def body(b, cur, prev, nxt):
                if prev:
                    dve.wait_ge(v3_mm, b.count(1, 0))
                    then(dve.tensor_tensor(out3[:, :], pw[:, 0:CC], k3[:, :], ALU.add))
                    then(dve.tensor_tensor(out3[:, :], out3[:, :], r3[:, :], ALU.mult))
                    dve.tensor_tensor(out3[:, :], out3[:, :], cb[:, :], ALU.add).then_inc(out3_ready, 1)
                if cur:
                    dve.wait_ge(xT_hi, b.count(1, 1))
                    dve.tensor_copy(xT[:, :, :], heads(pt[:, 0:CC * T], CC)).then_inc(xT_copy, 1)
                    dve.wait_ge(xT_copy, b.count(1, 1))
                    dve.tensor_tensor(xTl[:, :, :], xT[:, :, :], xTh[:, :, :].bitcast(F32), ALU.subtract).then_inc(xT_lo, 1)
                    dve.tensor_reduce(xsum[:, :], xT[:, :, :], AX.X, ALU.add).then_inc(sum_ready, 1)
                    for n in range(QB):
                        dve.wait_ge(qk_mm, b.count(QB, n + 1))
                        dve.tensor_tensor(qk[:, D * n:D * n + D], pp[0:T, n % 2, :],
                                          bias_qk[:, D * n:D * n + D], ALU.add).then_inc(qk_ready, 1)
                    dve.wait_ge(sq_ready, b.count(QB, QB))
                    then(dve.tensor_reduce(ss[:, :], rq3, AX.X, ALU.add))
                    dve.tensor_scalar(ss[:, 0:NL * NH], ss[:, 0:NL * NH], 1.0 / DH, RMS_EPS,
                                      ALU.mult, ALU.add).then_inc(ss_ready, 1)
                    dve.wait_ge(norm_ready, b.count(1, 1))
                    then(dve.tensor_tensor(qk3, qk3, ss[:, :].unsqueeze(2).broadcast_to((T, HEADS, DH)), ALU.mult))
                    order.mark(dve.tensor_tensor(t3, odd, sin3, ALU.mult))
                    order.mark(dve.tensor_tensor(first, even, cos3, ALU.mult))
                    then(dve.tensor_tensor(second, even, sin3, ALU.mult))
                    then(dve.tensor_tensor(first, first, t3, ALU.subtract))
                    then(dve.tensor_tensor(t3, odd, cos3, ALU.mult))
                    dve.tensor_tensor(second, second, t3, ALU.add).then_inc(roped, 1)
                if prev:
                    if cur:
                        dve.wait_ge(roped, b.count(1, 1))
                    dve.wait_ge(pv_mm, b.count(1, 0))
                    pv = pq[0:T, :, 0:PV].rearrange("p k (n d) -> p k n d", d=DH + 1)
                    then(dve.tensor_scalar(rden[:, :].rearrange("p (k n) -> p k n", k=4), pv[:, :, :, DH],
                                           float(NBR), None, ALU.mult))
                    then(dve.reciprocal(rden[:, :], rden[:, :]))
                    t4 = tmp[:, :].rearrange("p (k n d) -> p k n d", k=4, d=DH)
                    n4 = HK * NL
                    for k in range(4):
                        ins = dve.tensor_tensor(t4[:, k], pv[:, k, :, 0:DH],
                                                rden[:, n4 * k:n4 * k + n4].unsqueeze(2).broadcast_to((T, n4, DH)), ALU.mult)
                        ins.then_inc(pv_used, 1)
                    dve.wait_ge(pv_used, b.count(4, 0))
                    t5 = tmp[:, :].rearrange("p (h n d) -> p n h d", h=NH, n=NL)
                    c3 = heads(ctxr[:, :], NH)
                    then(dve.tensor_tensor(c3, t5[:, 0], t5[:, 1], ALU.add))
                    dve.tensor_tensor(c3, c3, t5[:, 2], ALU.add).then_inc(ctx_ready, 1)
                if cur:
                    for g in range(QC // 4):
                        dve.wait_ge(hT_hi, b.count(QC // 4, g + 1))
                        dve.tensor_tensor(qkTl[:, 4 * g:4 * g + 4, :], heads(pp[:, (QB + NL + g) % 2, 0:4 * T], 4),
                                          qkTh[:, 4 * g:4 * g + 4, :].bitcast(F32), ALU.subtract).then_inc(hT_lo, 1)
                if nxt:
                    need(dve, xT_mm, b.count(1, 1))
                    dve.wait_ge(x_in, b.count(16, 32))
                    row_stats(dve, order, xin[:, :], stats[:, :], mv[:, :], var_ready)
                    dve.wait_ge(rstd_ready, b.count(1, 2))
                    dve.tensor_scalar(xn[:, :], xin[:, :], mv[:, 0:1], rstd[:, :],
                                      ALU.subtract, ALU.mult).then_inc(xn_ready, 1)
                if prev:
                    dve.wait_ge(cT_mm, b.count(1, 0))
                    dve.wait_ge(out3_ready, b.count(1, 0))
                    dve.tensor_tensor(ctxT[:, :, :], heads(pt[:, 0:CC * T], CC),
                                      out3[:, :].unsqueeze(2).broadcast_to((128, CC, T)), ALU.add).then_inc(cT_ready, 1)
                    need(dve, x1_out, b.count(16, -16))
                    dve.wait_ge(xres_ready, b.count(1, 0))
                    dve.wait_ge(y_mm, b.count(1, 0))
                    dve.tensor_tensor(x1[:, :], pw[0:T, :], xres[:, :], ALU.add).then_inc(x1_ready, 1)
                order.finish()
            each_batch(dve, body)

        @block.tensor
        def _(pe):
            pe.wait_ge(lo_made, len(UNITS))

            def body(b, cur, prev, nxt):
                if prev:
                    pe.wait_ge(sum_ready, b.count(1, 0))
                    need(pe, x1_ready, b.count(1, -1))
                    for o in range(CC):
                        for c in range(CC):
                            last = pe.matmul(pw[:, o:o + 1], Wv[:, c, NQ + 128 * o:NQ + 128 * o + 128],
                                             xsum[:, c:c + 1], start=c == 0, stop=c == CC - 1)
                    last.then_inc(v3_mm, 1)
                if cur:
                    pe.wait_ge(xn_ready, b.count(1, 1))
                    need(pe, cT_ready, b.count(1, -1))
                    for c in range(CC):
                        last = pe.transpose(pt[:, T * c:T * c + T], xn[:, 128 * c:128 * c + 128], ident[0:T, 0:T])
                    last.then_inc(xT_mm, 1)
                    pe.wait_ge(xT_lo, b.count(1, 1))
                    for n in range(QB):
                        if n < 2:
                            need(pe, hT_lo, b.count(QC // 4, -n))
                        else:
                            pe.wait_ge(qk_ready, b.count(QB, n - 1))
                        cols = slice(D * n, D * n + D)
                        for c in range(CC):
                            last = split3(pe, pp[0:T, n % 2, :], xTh[:, c, :], xTl[:, c, :],
                                          WqkH[:, c, cols], WqkL[:, c, cols], c == 0, c == CC - 1)
                        last.then_inc(qk_mm, 1)
                if prev:
                    pe.wait_ge(v_ready, b.count(NL, 0))
                    pe.wait_ge(masked, b.count(1, 0))
                    for h in range(NH):
                        for br in range(NL):
                            at = ((h % HK) * NL + br) * (DH + 1)
                            last = pe.matmul(pq[0:T, h // HK, at:at + DH + 1], E[:, h, br, :], V[:, h, br, :],
                                             start=True, stop=True)
                    last.then_inc(pv_mm, 1)
                if cur:
                    for br in range(NL):
                        if br < 2:
                            pe.wait_ge(qk_ready, b.count(QB, QB - 1 + br))
                        else:
                            pe.wait_ge(v_ready, b.count(NL, br - 1))
                        for c in range(CC):
                            last = pe.matmul(pp[0:T, (QB + br) % 2, :], xT[:, c, :], Wv[:, c, D * br:D * br + D],
                                             start=c == 0, stop=c == CC - 1)
                        last.then_inc(v_mm, 1)
                    pe.wait_ge(roped, b.count(1, 1))
                    for g in range(QC // 4):
                        if g < 2:
                            pe.wait_ge(v_ready, b.count(NL, NL - 1 + g))
                        else:
                            pe.wait_ge(hT_lo, b.count(QC // 4, g - 1))
                        for i in range(4):
                            last = pe.transpose(pp[:, (QB + NL + g) % 2, T * i:T * i + T],
                                                rq[:, 128 * (4 * g + i):128 * (4 * g + i) + 128], ident[0:T, 0:T])
                        last.then_inc(hT_mm, 1)
                    pe.wait_ge(hT_lo, b.count(QC // 4, QC // 4))
                    for h in range(NH):
                        if h < 4:
                            need(pe, pv_used, b.count(4, 0))
                        else:
                            pe.wait_ge(e_ready, b.count(NH, h - 3))
                        rows, g = slice(DH * (h % 4), DH * (h % 4) + DH), h // 4
                        q = lambda t: t[rows, g:NL * 4:4, :]
                        k = lambda t: t[rows, NL * 4 + g, :]
                        split3(pe, heads(pq[0:T, h % 4, 0:NL * T], NL), k(qkTh), k(qkTl), q(qkTh), q(qkTl),
                               True, True).then_inc(s_mm, 1)
                if prev:
                    pe.wait_ge(ctx_ready, b.count(1, 0))
                    for c in range(CC):
                        last = pe.transpose(pt[:, T * c:T * c + T], ctxr[:, 128 * c:128 * c + 128], ident[0:T, 0:T])
                    last.then_inc(cT_mm, 1)
                    pe.wait_ge(cT_ready, b.count(1, 0))
                    for c in range(CC):
                        last = pe.matmul(pw[0:T, :], ctxT[:, c, :], WO[:, c, :], start=c == 0, stop=c == CC - 1)
                    last.then_inc(y_mm, 1)
            each_batch(pe, body)


class Tile:

    REST = 4 * T - 3 * 128

    def __init__(self, i):
        self.i = i
        self.rest = i == 12
        self.g, self.t = divmod(i, 3)
        self.rows = 4 * self.REST if self.rest else 128
        self.dims = 128 if self.rest else 2 * DH

    def blocks(self):
        if self.rest:
            return [(DH * g, slice(self.REST * g, self.REST * (g + 1)), 3 * DH, g, slice(T - self.REST, T))
                    for g in range(4)]
        out = []
        for n in range(2):
            h = self.t + n
            lo, hi = max(128 * self.t, T * h), min(128 * self.t + 128, T * h + T)
            out.append((DH * n, slice(lo - 128 * self.t, hi - 128 * self.t), DH * h, self.g, slice(lo - T * h, hi - T * h)))
        return out


def cross_program(nc, A, M, x1_dram, out_dram):
    NT = 13
    STEPS = [[Tile(i) for i in range(NT)][2 * s:2 * s + 2] for s in range(7)]
    TILES = [t for s in STEPS for t in s]
    KC = 6
    HALF = 3 * 128
    HALVES = [(0, HALF), (HALF, KV - HALF)]
    KEY0 = [128 * k for k in range(KC - 1)] + [KV - 128]
    SPLIT = 150
    RING = 4
    SLICES = [(half, kind, n) for half in range(2) for kind, n in
              [("K", g) for g in range(4)] + [("V", 3 * half + k) for k in range(3)]]
    NSL = len(SLICES)
    PLAN = [([12, 13], []), ([], [0, 1]), ([2, 3], [4]), ([5, 6], []), ([], [7, 8]), ([9], [10]), ([11], [])]
    assert [n for a, b in PLAN[1:] + PLAN[:1] for n in a + b] == list(range(NSL))
    with ExitStack() as ctx:
        sb = lambda n, s, d=F32: ctx.enter_context(nc.sbuf_tensor("ca_" + n, s, d))
        ps = lambda n, s: ctx.enter_context(nc.psum_tensor("ca_" + n, s, F32))
        sem = lambda n: ctx.enter_context(nc.semaphore("ca_" + n))
        chunks = lambda t, n: t.rearrange("p (c d) -> p c d", c=n)
        WkH, WkL, WvH, WvL = (sb(n, [128, CC, D], F32R) for n in ("WkH", "WkL", "WvH", "WvL"))
        WqT, WoT = sb("WqT", [128, CC, D]), sb("WoT", [128, CC, D])
        ident = sb("ident", [128, 128])
        tail_keys = sb("tail_keys", [128, 1])
        bq, bk, bv = (sb(n, [128, CC]) for n in ("bq", "bk", "bv"))
        bias_o, bias_f = sb("bias_o", [T, D]), sb("bias_f", [T, D])
        minus_half = sb("minus_half", [T, 1])
        raw = sb("raw", [128, 2, HALF])
        cH, cL = sb("cH", [128, CC, HALF], F32R), sb("cL", [128, CC, HALF], F32R)
        K32 = sb("K32", [128, HALF])
        KH = [sb(f"KH{p}", [128, CC, KV], F32R) for p in range(2)]
        KL = [sb(f"KL{p}", [128, CC, KV], F32R) for p in range(2)]
        V = [sb(f"V{p}", [128, KC, D]) for p in range(2)]
        QH, QL = sb("QH", [128, CC, 4 * T], F32R), sb("QL", [128, CC, 4 * T], F32R)
        REST = Tile.REST
        RH, RL = (sb(n, [128, 5 * 4 * REST], F32R) for n in ("RH", "RL"))
        S = [sb(f"S{r}", [128, KV]) for r in range(RING)]
        E = [sb(f"E{r}", [128, KV]) for r in range(RING)]
        W = [sb(f"W{r}", [128, KV]) for r in range(2)]
        top = [sb(f"top{r}", [128, TOPK]) for r in range(RING)]
        shift, Z, rZ = (sb(n, [128, RING]) for n in ("shift", "Z", "rZ"))
        PT = sb("PT", [128, KC, 128])
        On = sb("On", [128, 128])
        ctxT = sb("ctxT", [128, CC, T])
        xin, xn, x2 = (sb(n, [T, D]) for n in ("xin", "xn", "x2"))
        xb = [sb(f"xb{p}", [T, D]) for p in range(2)]
        stats, mv, rstd = sb("stats", [T, 6]), sb("mv", [T, 2]), sb("rstd", [T, 1])
        xT = sb("xT", [128, CC, T])
        pS, pT = ps("pS", [128, 1024]), ps("pT", [128, 1024])
        pO, pF, pX = ps("pO", [128, 512]), ps("pF", [128, 2, 512]), ps("pX", [128, 512])
        scores = pS[:, SPLIT:SPLIT + KV]

        setup_in, w_in, w_hi, w_lo = sem("setup_in"), sem("w_in"), sem("w_hi"), sem("w_lo")
        zeroed, bias_mm, bias_ready = sem("zeroed"), sem("bias_mm"), sem("bias_ready")
        dve_order, pool_order, act_order = sem("dve_order"), sem("pool_order"), sem("act_order")
        ctx_in, x_in, out_done = sem("ctx_in"), sem("x_in"), sem("out_done")
        ctx_hi, ctx_lo = sem("ctx_hi"), sem("ctx_lo")
        kv_mm, kv_out, k_hi, k_lo = sem("kv_mm"), sem("kv_out"), sem("k_hi"), sem("k_lo")
        var1_ready, rstd1_ready, xn1_ready, x1T_mm, x1T_ready = (
            sem(n) for n in ("var1_ready", "rstd1_ready", "xn1_ready", "x1T_mm", "x1T_ready"))
        var2_ready, rstd2_ready, xn2_ready, x2T_mm, x2T_ready = (
            sem(n) for n in ("var2_ready", "rstd2_ready", "xn2_ready", "x2T_mm", "x2T_ready"))
        xb_ready = sem("xb_ready")
        q_mm, q_ready, q_hi, q_lo = sem("q_mm"), sem("q_ready"), sem("q_hi"), sem("q_lo")
        s_mm, s_ready, shift_ready, e_ready = sem("s_mm"), sem("s_ready"), sem("shift_ready"), sem("e_ready")
        picked, f_ready, z_ready, rz_ready, p_ready = (sem(n) for n in ("picked", "f_ready", "z_ready", "rz_ready", "p_ready"))
        pt_mm, pt_ready, o_mm, o_ready, ot_mm, ot_ready = (
            sem(n) for n in ("pt_mm", "pt_ready", "o_mm", "o_ready", "ot_mm", "ot_ready"))
        y_mm, x2_ready, x2f_ready, f_mm, out_ready = (sem(n) for n in ("y_mm", "x2_ready", "x2f_ready", "f_mm", "out_ready"))

        SETUP = [(WqT[:, :, :], A["WqT"].rearrange("(c p) o -> p c o", p=128)),
                 (WoT[:, :, :], A["WoT"].rearrange("(c p) o -> p c o", p=128)),
                 (ident[:, :], A["ident"]), (tail_keys[:, :], A["tail_keys"]),
                 (bq[:, :], A["xbq"]), (bk[:, :], A["xbk"]), (bv[:, :], A["xbv"]),
                 (bias_o[:, :], A["xbo"][0:1, :].broadcast_to((T, D))),
                 (bias_f[:, :], A["ffn_bias"][0:1, :].broadcast_to((T, D)))]
        WSPLIT = [(A["WkT"], WkH, WkL, c) for c in range(CC)] + [(A["WvT"], WvH, WvL, c) for c in range(CC)]

        def ring(t, b_par):
            return (t.i + 2 * b_par) % RING

        def before(b, t, n):
            if t.i >= n:
                return b, t.i - n
            return b.next(-1), ({0: 10, 1: 11, 2: 12, 3: 9}[t.i] if n == 4 else NT - n + t.i)

        def each_batch(eng, body):
            body(At(-1), 1, tiles=False, prev=False, nxt=True)
            body(At(0), 0, tiles=True, prev=False, nxt=True)
            with eng.Fori(0, (B - 2) // 2) as i:
                body(At(1, i, 2), 1, tiles=True, prev=True, nxt=True)
                body(At(2, i, 2), 0, tiles=True, prev=True, nxt=True)
            body(At(B - 1), 1, tiles=True, prev=True, nxt=False)
            body(At(B), 0, tiles=False, prev=True, nxt=False)

        def batch_of(dram, b, n):
            i = b.const + n if b.reg is None else b.reg * b.factor + (b.const + n)
            return dram[bass.ds(i, 1)].rearrange("o t d -> (o t) d")

        def tiles_at(s, b, par, tiles, prev, nxt):
            nb, np_ = b.next(1), 1 - par
            pb = b.next(-1)
            cur = [(b, par, t) for t in STEPS[s]] if tiles else []
            if s:
                last = [(b, par, t) for t in STEPS[s - 1]] if tiles else []
            else:
                last = [(pb, 1 - par, t) for t in STEPS[6]] if prev else []
            if s < 6:
                coming = [(b, par, t) for t in STEPS[s + 1]] if tiles else []
            else:
                coming = [(nb, np_, t) for t in STEPS[0]] if nxt else []
            return cur, last, coming

        def late_tile(s, b, par, tiles, prev):
            if s == 0:
                return [(b.next(-1), 1 - par, STEPS[5][1])] if prev else []
            return [(b, par, STEPS[s - 2][1])] if s > 1 and tiles else []

        def slices(s, part, b, par, tiles, nxt):
            if s == 0:
                return [(b, par, n) for n in PLAN[s][part]] if tiles else []
            return [(b.next(), 1 - par, n) for n in PLAN[s][part]] if nxt else []

        block = ctx.enter_context(nc.Block())

        @block.sync
        def _(sp):
            for t, a in SETUP:
                sp.dma_start(t, a).then_inc(setup_in, 16)
            for u, (w, _, _, c) in enumerate(WSPLIT):
                sp.dma_start(E[u % 4][:, 0:D] if u < 4 else S[u % 4][:, 0:D], w[128 * c:128 * c + 128, :]).then_inc(w_in, 16)

            def load_context(b, half):
                k0, kn = HALVES[half]
                i = b.const + 1 if b.reg is None else b.reg * b.factor + (b.const + 1)
                for piece in range(2):
                    need(sp, ctx_hi, b.next().count(4, 2 * half + piece))
                    need(sp, ctx_lo, b.next().count(4, 2 * half + piece))
                    src = A["ctxT"][bass.ds(i, 1), 256 * piece:256 * piece + 256, k0:k0 + kn]
                    sp.dma_start(raw[:, :, 0:kn], src.rearrange("o (c p) k -> p (o c) k", p=128)).then_inc(ctx_in, 16)

            def body(b, par, tiles, prev, nxt):
                if nxt:
                    load_context(b, 0)
                    load_context(b, 1)
                    need(sp, xn1_ready, b.count(1, 1))
                    need(sp, xb_ready, b.count(1, 1))
                    sp.dma_start(xin[:, :], batch_of(x1_dram, b, 1)).then_inc(x_in, 16)
                if prev:
                    sp.wait_ge(out_ready, b.count(1, 0))
                    sp.dma_start(batch_of(out_dram, b, -1), x2[:, :]).then_inc(out_done, 16)
            each_batch(sp, body)
            sp.wait_ge(out_done, 16 * B)

        @block.gpsimd
        def _(pool):
            for t in (QH[:, :, :], QL[:, :, :], RH[:, :], RL[:, :]):
                pool.memset(t.bitcast(F32), 0.0).then_inc(zeroed, 1)
            order = Order(pool, pool_order)
            order.mark(pool.memset(minus_half[:, :], -0.5))
            order.finish()

            def key_low(bn, pn, n):
                half, _, g = SLICES[n]
                k0, kn = HALVES[half]
                i = 4 * half + g
                pool.wait_ge(k_hi, bn.count(8, i + 1))
                pool.tensor_tensor(KL[pn][:, g, k0:k0 + kn], K32[:, 0:kn],
                                   KH[pn][:, g, k0:k0 + kn].bitcast(F32), ALU.subtract).then_inc(k_lo, 1)

            def context_low(bn, piece):
                kn, cs = HALVES[piece // 2][1], slice(2 * (piece % 2), 2 * (piece % 2) + 2)
                if piece % 2 == 0:
                    need(pool, kv_mm, bn.count(NSL, 7 * (piece // 2)))
                pool.wait_ge(ctx_hi, bn.count(4, piece + 1))
                pool.tensor_tensor(cL[:, cs, 0:kn], raw[:, :, 0:kn], cH[:, cs, 0:kn].bitcast(F32),
                                   ALU.subtract).then_inc(ctx_lo, 1)

            def body(b, par, tiles, prev, nxt):
                bn, pn = b.next(), 1 - par
                for s in range(7):
                    cur, last, coming = tiles_at(s, b, par, tiles, prev, nxt)
                    for tb, tp, t in last:
                        r = ring(t, tp)
                        pool.wait_ge(f_ready, tb.count(NT, t.i + 1))
                        pool.tensor_tensor(E[r][0:t.rows, :], E[r][0:t.rows, :], S[r][0:t.rows, :],
                                           ALU.subtract).then_inc(p_ready, 1)
                    if s == 2 and prev:
                        pool.wait_ge(var2_ready, b.count(1, 0))
                        pool.tensor_tensor(rstd[:, :], mv[:, 1:2], minus_half[:, :], ALU.pow).then_inc(rstd2_ready, 1)
                    if s == 3 and prev:
                        pool.wait_ge(xn2_ready, b.count(1, 0))
                        pool.tensor_tensor(x2[:, :], x2[:, :], bias_f[:, :], ALU.add).then_inc(x2f_ready, 1)
                    if s == 4 and nxt:
                        pool.wait_ge(var1_ready, bn.count(1, 1))
                        pool.tensor_tensor(rstd[:, :], mv[:, 1:2], minus_half[:, :], ALU.pow).then_inc(rstd1_ready, 1)
                        pool.wait_ge(bias_ready, 1)
                        pool.tensor_tensor(xb[pn][:, :], xin[:, :], bias_o[:, :], ALU.add).then_inc(xb_ready, 1)
                    if s in (0, 1, 3, 4) and nxt:
                        context_low(bn, 2 * (s // 3) + s % 3)
                    for x in slices(s, 0, b, par, tiles, nxt) + slices(s, 1, b, par, tiles, nxt):
                        if SLICES[x[2]][1] == "K":
                            key_low(*x)
                order.finish()
            each_batch(pool, body)

        @block.tensor
        def _(pe):
            pe.wait_ge(setup_in, 16 * len(SETUP))
            pe.wait_ge(zeroed, 5)
            for c in range(CC):
                last = pe.matmul(pX[0:T, :], xT[:, c, :], WoT[:, c, :], start=c == 0, stop=c == CC - 1)
            last.then_inc(bias_mm, 1)
            pe.wait_ge(bias_ready, 1)
            pe.wait_ge(w_lo, len(WSPLIT))

            def project(bn, pn, n):
                half, kind, k = SLICES[n]
                k0, kn = HALVES[half]
                if n % 7 == 0:
                    pe.wait_ge(ctx_lo, bn.count(4, 2 * half + 2))
                need(pe, kv_out, bn.count(NSL, n - 1))
                for c in range(CC):
                    if kind == "K":
                        cols = slice(128 * k, 128 * k + 128)
                        last = split3(pe, pF[:, n % 2, 0:kn], WkH[:, c, cols], WkL[:, c, cols],
                                      cH[:, c, 0:kn], cL[:, c, 0:kn], c == 0, c == CC - 1)
                    else:
                        keys = slice(KEY0[k] - k0, KEY0[k] - k0 + 128)
                        last = split3(pe, pF[:, n % 2, :], cH[:, c, keys], cL[:, c, keys],
                                      WvH[:, c, :], WvL[:, c, :], c == 0, c == CC - 1)
                last.then_inc(kv_mm, 1)

            def transposed(x, done):
                for c in range(CC):
                    last = pe.transpose(pX[:, T * c:T * c + T], x[:, 128 * c:128 * c + 128], ident[0:T, 0:T])
                last.then_inc(done, 1)

            def score(tb, tp, t):
                if t.i == 0:
                    pe.wait_ge(q_lo, tb.count(5, 5))
                if t.t == 0 or t.rest:
                    pe.wait_ge(k_lo, tb.count(8, 5 + min(t.g, 3)))
                need(pe, s_ready, tb.count(NT, t.i))
                parts = [(slice(0, 512 - SPLIT), slice(SPLIT, 512)), (slice(512 - SPLIT, KV), slice(512, KV + SPLIT))]
                for keys, cols in parts:
                    out = pS[0:t.rows, cols]
                    if t.rest:
                        for g in range(4):
                            rows = slice(t.rows * g, t.rows * g + t.rows)
                            last = split3(pe, out, RH[:, rows], RL[:, rows], KH[tp][:, g, keys], KL[tp][:, g, keys],
                                          g == 0, g == 3)
                    else:
                        rows = slice(128 * t.t, 128 * t.t + 128)
                        last = split3(pe, out, QH[:, t.g, rows], QL[:, t.g, rows],
                                      KH[tp][:, t.g, keys], KL[tp][:, t.g, keys], True, True)
                last.then_inc(s_mm, 1)

            def weights_T(tb, tp, t):
                pe.wait_ge(p_ready, tb.count(NT, t.i + 1))
                need(pe, pt_ready, tb.count(NT, t.i))
                settle(pe)
                for k in range(KC):
                    last = pe.transpose(pT[:, 128 * k:128 * k + t.rows],
                                        E[ring(t, tp)][0:t.rows, KEY0[k]:KEY0[k] + 128], ident[0:t.rows, 0:t.rows])
                last.then_inc(pt_mm, 1)

            def values(tb, tp, t):
                pe.wait_ge(pt_ready, tb.count(NT, t.i + 1))
                need(pe, ot_ready, tb.count(NT, t.i))
                if t.i == 0:
                    pe.wait_ge(kv_out, tb.count(NSL, NSL))
                for k in range(KC):
                    if t.rest:
                        rhs = V[tp][:, k, :].rearrange("p (g h d) -> p g h d", g=4, h=4)[:, :, 3, :]
                    else:
                        h = 4 * t.g + t.t
                        rhs = V[tp][:, k, DH * h:DH * h + t.dims]
                    out = pO[0:t.rows, 0:t.dims]
                    if t.rest:
                        out = out.rearrange("p (g d) -> p g d", g=4)
                    last = pe.matmul(out, PT[:, k, 0:t.rows], rhs, start=k == 0, stop=k == KC - 1)
                last.then_inc(o_mm, 1)

            def output_T(tb, tp, t):
                pe.wait_ge(o_ready, tb.count(NT, t.i + 1))
                settle(pe)
                pe.transpose(pO[0:t.dims, 256:256 + t.rows], On[0:t.rows, 0:t.dims],
                             ident[0:t.rows, 0:t.rows]).then_inc(ot_mm, 1)

            def body(b, par, tiles, prev, nxt):
                bn = b.next()
                for s in range(7):
                    cur, last, coming = tiles_at(s, b, par, tiles, prev, nxt)
                    if s == 1 and prev:
                        pe.wait_ge(ot_ready, b.count(NT, 0))
                        for c in range(CC):
                            ins = pe.matmul(pX[0:T, :], ctxT[:, c, :], WoT[:, c, :], start=c == 0, stop=c == CC - 1)
                        ins.then_inc(y_mm, 1)
                    if s == 3 and prev:
                        pe.wait_ge(xn2_ready, b.count(1, 0))
                        transposed(xn, x2T_mm)
                    if s == 4 and prev:
                        pe.wait_ge(x2T_ready, b.count(1, 0))
                        for c in range(CC):
                            ins = pe.matmul(pX[0:T, :], xT[:, c, :], M[:, c, :], start=c == 0, stop=c == CC - 1)
                        ins.then_inc(f_mm, 1)
                    if coming and s < 6:
                        score(*coming[0])
                    for x in late_tile(s, b, par, tiles, prev):
                        values(*x)
                    for x in slices(s, 0, b, par, tiles, nxt):
                        project(*x)
                    if last:
                        weights_T(*last[0])
                    for x in late_tile(s, b, par, tiles, prev):
                        output_T(*x)
                    if coming and s == 6:
                        score(*coming[0])
                    if len(coming) > 1:
                        score(*coming[1])
                    if s == 5 and nxt:
                        need(pe, out_ready, b.count(1, 0))
                        pe.wait_ge(xn1_ready, bn.count(1, 1))
                        transposed(xn, x1T_mm)
                    if last:
                        values(*last[0])
                    if len(last) > 1:
                        weights_T(*last[1])
                    for x in slices(s, 1, b, par, tiles, nxt):
                        project(*x)
                    if s == 5 and nxt:
                        pe.wait_ge(x1T_ready, bn.count(1, 1))
                        for o in range(CC):
                            for c in range(CC):
                                ins = pe.matmul(pX[:, T * o:T * o + T], WqT[:, c, 128 * o:128 * o + 128], xT[:, c, :],
                                                start=c == 0, stop=c == CC - 1)
                        ins.then_inc(q_mm, 1)
                    if last:
                        output_T(*last[0])
            each_batch(pe, body)

        @block.scalar
        def _(act):
            for u, (_, wh, _, c) in enumerate(WSPLIT):
                src = E[u % 4] if u < 4 else S[u % 4]
                act.wait_ge(w_in, 16 * len(WSPLIT))
                act.activation(wh[:, c, :], src[:, 0:D], ACT.Copy).then_inc(w_hi, 1)
            act.wait_ge(setup_in, 16 * len(SETUP))
            act.wait_ge(w_lo, len(WSPLIT))
            act.wait_ge(zeroed, 5)

            def context_high(bn, piece):
                kn, cs = HALVES[piece // 2][1], slice(2 * (piece % 2), 2 * (piece % 2) + 2)
                if piece % 2 == 0:
                    need(act, kv_mm, bn.count(NSL, 7 * (piece // 2)))
                act.wait_ge(ctx_in, bn.count(64, 16 * (piece + 1)))
                act.activation(cH[:, cs, 0:kn], raw[:, :, 0:kn], ACT.Copy).then_inc(ctx_hi, 1)

            def keep(bn, pn, n):
                half, kind, k = SLICES[n]
                act.wait_ge(kv_mm, bn.count(NSL, n + 1))
                if kind == "V":
                    scale = tail_keys[:, 0:1] if k == KC - 1 else 1.0
                    act.activation(V[pn][:, k, :], pF[:, n % 2, :], ACT.Copy, scale=scale).then_inc(kv_out, 1)
                    return
                k0, kn = HALVES[half]
                i = 4 * half + k
                need(act, k_lo, bn.count(8, i))
                act.activation(K32[:, 0:kn], pF[:, n % 2, 0:kn], ACT.Identity,
                               bias=bk[:, k:k + 1]).then_inc(kv_out, 1)
                act.wait_ge(kv_out, bn.count(NSL, n + 1))
                act.activation(KH[pn][:, k, k0:k0 + kn], K32[:, 0:kn], ACT.Copy).then_inc(k_hi, 1)

            def exps_left(tb, tp, t):
                r, rows = ring(t, tp), slice(0, t.rows)
                act.wait_ge(picked, tb.count(NT, t.i + 1))
                act.wait_ge(e_ready, tb.count(NT, t.i + 1))
                act.activation(S[r][rows, :], W[(t.i + tp) % 2][rows, :], ACT.Exp, bias=shift[rows, r:r + 1],
                               scale=SCALE).then_inc(f_ready, 1)
                act.activation(top[r][rows, :], top[r][rows, :], ACT.Exp, bias=shift[rows, r:r + 1],
                               scale=SCALE, accum_out=Z[rows, r:r + 1]).then_inc(z_ready, 1)

            def exps(tb, tp, t):
                r, rows = ring(t, tp), slice(0, t.rows)
                ob, oi = before(tb, t, RING)
                need(act, pt_mm, ob.count(NT, oi + 1))
                act.wait_ge(shift_ready, tb.count(NT, t.i + 1))
                act.activation(E[r][rows, :], S[r][rows, :], ACT.Exp, bias=shift[rows, r:r + 1],
                               scale=SCALE).then_inc(e_ready, 1)

            def keep_scores(tb, tp, t):
                ob, oi = before(tb, t, RING)
                need(act, p_ready, ob.count(NT, oi + 1))
                act.wait_ge(s_mm, tb.count(NT, t.i + 1))
                act.activation(S[ring(t, tp)][0:t.rows, :], scores[0:t.rows, :], ACT.Copy).then_inc(s_ready, 1)

            def keep_weights_T(tb, tp, t):
                need(act, o_mm, tb.count(NT, t.i))
                act.wait_ge(pt_mm, tb.count(NT, t.i + 1))
                act.activation(PT[:, :, 0:t.rows], chunks(pT[:, 0:KC * 128], KC)[:, :, 0:t.rows],
                               ACT.Copy).then_inc(pt_ready, 1)

            def normalise(tb, tp, t):
                r = ring(t, tp)
                act.wait_ge(rz_ready, tb.count(NT, t.i + 1))
                act.wait_ge(o_mm, tb.count(NT, t.i + 1))
                need(act, ot_mm, tb.count(NT, t.i))
                act.activation(On[0:t.rows, 0:t.dims], pO[0:t.rows, 0:t.dims], ACT.Copy,
                               scale=rZ[0:t.rows, r:r + 1]).then_inc(o_ready, 1)

            def place_output(tb, tp, t):
                if t.i == 0:
                    need(act, y_mm, tb.count(1, 0))
                act.wait_ge(ot_mm, tb.count(NT, t.i + 1))
                for p, cols, to, g, q in t.blocks():
                    ins = act.activation(ctxT[to:to + DH, g, q], pO[p:p + DH, 256 + cols.start:256 + cols.stop], ACT.Copy)
                ins.then_inc(ot_ready, 1)

            def body(b, par, tiles, prev, nxt):
                bn, pn = b.next(), 1 - par
                for s in range(7):
                    cur, last, coming = tiles_at(s, b, par, tiles, prev, nxt)
                    for x in last:
                        exps_left(*x)
                    if s == 6 and nxt:
                        need(act, s_mm, b.count(NT, NT))
                        act.wait_ge(q_ready, bn.count(1, 1))
                        for h in range(4):
                            rows = slice(DH * h, DH * h + DH)
                            act.activation(QH[rows, :, T * h:T * h + T], xT[rows, :, :], ACT.Copy).then_inc(q_hi, 1)
                        act.activation(chunks(RH[3 * DH:128, :], 4)[:, :, 0:REST], xT[3 * DH:128, :, T - REST:T],
                                       ACT.Copy).then_inc(q_hi, 1)
                    for x in cur:
                        exps(*x)
                    if s == 3 and prev:
                        act.wait_ge(x2T_mm, b.count(1, 0))
                        act.activation(xT[:, :, :], chunks(pX[:, 0:CC * T], CC), ACT.Copy).then_inc(x2T_ready, 1)
                    if s in (1, 4) and nxt:
                        context_high(bn, 2 * (s // 3) + 1)
                    if coming and s < 6:
                        keep_scores(*coming[0])
                    for x in late_tile(s, b, par, tiles, prev):
                        normalise(*x)
                    for x in slices(s, 0, b, par, tiles, nxt):
                        keep(*x)
                    if last:
                        keep_weights_T(*last[0])
                    for x in late_tile(s, b, par, tiles, prev):
                        place_output(*x)
                    if s in (0, 3) and nxt:
                        context_high(bn, 2 * (s // 3))
                    if coming and s == 6:
                        keep_scores(*coming[0])
                    if len(coming) > 1:
                        keep_scores(*coming[1])
                    if s == 5 and nxt:
                        act.wait_ge(x1T_mm, bn.count(1, 1))
                        act.activation(xT[:, :, :], chunks(pX[:, 0:CC * T], CC), ACT.Copy).then_inc(x1T_ready, 1)
                    if last:
                        normalise(*last[0])
                    if len(last) > 1:
                        keep_weights_T(*last[1])
                    for x in slices(s, 1, b, par, tiles, nxt):
                        keep(*x)
                    if last:
                        place_output(*last[0])
            each_batch(act, body)

        @block.vector
        def _(dve):
            order = Order(dve, dve_order)
            dve.wait_ge(setup_in, 16 * len(SETUP))
            dve.tensor_copy(xT[:, :, :], bv[:, :].unsqueeze(2).broadcast_to((128, CC, T))).then_inc(zeroed, 1)
            for u, (_, wh, wl, c) in enumerate(WSPLIT):
                src = E[u % 4] if u < 4 else S[u % 4]
                dve.wait_ge(w_hi, u + 1)
                dve.tensor_tensor(wl[:, c, :], src[:, 0:D], wh[:, c, :].bitcast(F32), ALU.subtract).then_inc(w_lo, 1)
            dve.wait_ge(bias_mm, 1)
            dve.tensor_tensor(bias_o[:, :], pX[0:T, :], bias_o[:, :], ALU.add).then_inc(bias_ready, 1)

            def body(b, par, tiles, prev, nxt):
                bn, pb = b.next(), b.next(-1)
                for s in range(7):
                    cur, last, coming = tiles_at(s, b, par, tiles, prev, nxt)
                    n_of = {}
                    if s == 6 and nxt:
                        dve.wait_ge(q_mm, bn.count(1, 1))
                        dve.tensor_tensor(xT[:, :, :], chunks(pX[:, 0:CC * T], CC),
                                          bq[:, :].unsqueeze(2).broadcast_to((128, CC, T)), ALU.add).then_inc(q_ready, 1)
                    for tb, tp, t in cur:
                        r, rows = ring(t, tp), slice(0, t.rows)
                        ob, oi = before(tb, t, RING)
                        need(dve, z_ready, ob.count(NT, oi + 1))
                        dve.wait_ge(s_ready, tb.count(NT, t.i + 1))
                        settle(dve)
                        order.after(max(order.n - 2, 0))
                        n_of[t.i] = order.mark(dve.max(top[r][rows, 0:8], S[r][rows, :]))
                    for tb, tp, t in cur:
                        r, rows = ring(t, tp), slice(0, t.rows)
                        order.after(n_of[t.i])
                        dve.tensor_scalar(shift[rows, r:r + 1], top[r][rows, 0:1], -SCALE, None,
                                          ALU.mult).then_inc(shift_ready, 1)
                    for k in range(TOPK // 8):
                        for tb, tp, t in cur:
                            r, rows, w = ring(t, tp), slice(0, t.rows), W[(t.i + tp) % 2]
                            eight = top[r][rows, 8 * k:8 * k + 8]
                            if k:
                                order.after(n_of[t.i])
                                n_of[t.i] = order.mark(dve.max(eight, w[rows, :]))
                        for tb, tp, t in cur:
                            r, rows, w = ring(t, tp), slice(0, t.rows), W[(t.i + tp) % 2]
                            eight = top[r][rows, 8 * k:8 * k + 8]
                            if k == 0:
                                ob, oi = before(tb, t, 2)
                                need(dve, f_ready, ob.count(NT, oi + 1))
                                settle(dve)
                            order.after(n_of[t.i])
                            ins = dve.match_replace(w[rows, :], eight, (w if k else S[r])[rows, :], REMOVED)
                            if k == TOPK // 8 - 1:
                                ins.then_inc(picked, 1)
                            else:
                                n_of[t.i] = order.mark(ins)
                        if k == 0:
                            for tb, tp, t in last:
                                r, rows = ring(t, tp), slice(0, t.rows)
                                dve.wait_ge(z_ready, tb.count(NT, t.i + 1))
                                dve.reciprocal(rZ[rows, r:r + 1], Z[rows, r:r + 1]).then_inc(rz_ready, 1)
                            if s == 2 and prev:
                                row_stats(dve, order, x2[:, :], stats[:, :], mv[:, :], var2_ready)
                            if s == 4 and nxt:
                                dve.wait_ge(x_in, bn.count(16, 16))
                                row_stats(dve, order, xin[:, :], stats[:, :], mv[:, :], var1_ready)
                        if k == 1 and s == 4 and prev:
                            dve.wait_ge(f_mm, b.count(1, 0))
                            dve.wait_ge(x2f_ready, b.count(1, 0))
                            dve.tensor_tensor(x2[:, :], pX[0:T, :], x2[:, :], ALU.add).then_inc(out_ready, 1)
                        if k == 0 and s == 6 and nxt:
                            lows = [(QH, QL, slice(DH * h, DH * h + DH), h) for h in range(4)]
                            for i, (qh, ql, rows, h) in enumerate(lows):
                                dve.wait_ge(q_hi, bn.count(5, i + 1))
                                dve.tensor_tensor(ql[rows, :, T * h:T * h + T], xT[rows, :, :],
                                                  qh[rows, :, T * h:T * h + T].bitcast(F32), ALU.subtract).then_inc(q_lo, 1)
                            dve.wait_ge(q_hi, bn.count(5, 5))
                            dve.tensor_tensor(chunks(RL[3 * DH:128, :], 4)[:, :, 0:REST], xT[3 * DH:128, :, T - REST:T],
                                              chunks(RH[3 * DH:128, :], 4)[:, :, 0:REST].bitcast(F32),
                                              ALU.subtract).then_inc(q_lo, 1)
                        if k == 2 and s == 1 and prev:
                            dve.wait_ge(y_mm, b.count(1, 0))
                            dve.wait_ge(xb_ready, b.count(1, 0))
                            need(dve, out_done, b.count(16, -16))
                            dve.tensor_tensor(x2[:, :], pX[0:T, :], xb[1 - par][:, :], ALU.add).then_inc(x2_ready, 1)
                            dve.wait_ge(x2_ready, b.count(1, 0))
                            settle(dve)
                        if k == 2 and s == 2 and prev:
                            need(dve, x1T_mm, b.count(1, 1) if nxt or tiles else b.count(1, 0))
                            dve.wait_ge(rstd2_ready, b.count(1, 0))
                            dve.tensor_scalar(xn[:, :], x2[:, :], mv[:, 0:1], rstd[:, :],
                                              ALU.subtract, ALU.mult).then_inc(xn2_ready, 1)
                        if k == 2 and s == 4 and nxt:
                            need(dve, x2T_mm, b.count(1, 0))
                            dve.wait_ge(rstd1_ready, bn.count(1, 1))
                            dve.tensor_scalar(xn[:, :], xin[:, :], mv[:, 0:1], rstd[:, :],
                                              ALU.subtract, ALU.mult).then_inc(xn1_ready, 1)
                order.finish()
            each_batch(dve, body)


def program(nc, A, out):
    x1_dram = nc.dram_tensor("x1_scratch", (B, T, D), F32, kind="Internal").ap()
    self_program(nc, A, x1_dram)
    with nc.sbuf_tensor("spectral_M", [128, CC, D], F32) as M:
        spectral_program(nc, A, M)
        cross_program(nc, A, M, x1_dram, out)


def kernel(**inputs):
    import concourse.bacc as bacc
    from concourse.bass_utils import run_bass_kernel_spmd

    a = {k: np.asarray(v) for k, v in inputs.items()}
    row = lambda v: np.ascontiguousarray(v).reshape(1, -1)
    cols = lambda v: np.ascontiguousarray(v.reshape(-1, 128).T)
    swap = lambda v: np.ascontiguousarray(np.swapaxes(v, -1, -2))
    f32 = lambda v: np.ascontiguousarray(v.astype(np.float32))
    n = np.arange(D)
    angle = 2.0 * np.pi * (np.outer(n, n) % D) / D
    freq = 1.0 / 10000.0 ** (np.arange(0, DH, 2) / DH)
    rope = np.arange(T)[:, None] * freq[None, :]
    arrays = {
        "cos": f32(np.cos(rope)), "sin": f32(np.sin(rope)), "ident": np.eye(128, dtype=np.float32),
        "dft_cos": f32(np.cos(angle)), "dft_sin": f32(np.sin(angle)), "dft_msin": f32(-np.sin(angle)),
        "tail_keys": f32((np.arange(128) >= 6 * 128 - KV).reshape(128, 1)),
        "x": a["x"], "ctxT": swap(a["ctx_1024"]),
        "WQ": a["L0_attn_WQ"], "bQ": row(a["L0_attn_bQ"]), "WK": a["L0_attn_WK"], "bK": row(a["L0_attn_bK"]),
        "WV": a["L0_attn_WV"], "bV": row(a["L0_attn_bV"]), "WO": a["L0_attn_WO"], "bO": row(a["L0_attn_bO"]),
        "sinks": row(a["L0_attn_sink_scalars"]), "v_nulls": row(a["L0_attn_v_nulls"]),
        "bV_cols": cols(a["L0_attn_bV"]), "v_nulls_cols": cols(a["L0_attn_v_nulls"]),
        "sinks_cols": cols(np.repeat(a["L0_attn_sink_scalars"], DH)),
        "WqT": swap(a["L0_xattn_Wq"]), "WkT": swap(a["L0_xattn_Wk"]),
        "WvT": swap(a["L0_xattn_Wv"]), "WoT": swap(a["L0_xattn_Wo"]),
        "xbq": cols(a["L0_xattn_bq"]), "xbk": cols(a["L0_xattn_bk"]),
        "xbv": cols(a["L0_xattn_bv"]), "xbo": row(a["L0_xattn_bo"]),
        "wrT": swap(a["L0_ffn_w_freq_real"]), "wiT": swap(a["L0_ffn_w_freq_imag"]),
        "ffn_bias": row(a["L0_ffn_bias"]),
    }
    nc = bacc.Bacc("TRN2", target_bir_lowering=False, num_devices=1)
    A = {k: nc.dram_tensor("in_" + k, v.shape, F32, kind="ExternalInput").ap() for k, v in arrays.items()}
    out = nc.dram_tensor("out", (B, T, D), F32, kind="ExternalOutput").ap()
    program(nc, A, out)
    r = run_bass_kernel_spmd(nc, [{"in_" + k: v for k, v in arrays.items()}], core_ids=[0])
    return r.results[0]["out"]
```

```python
from contextlib import ExitStack

import numpy as np
import concourse.bass as bass
import concourse.mybir as mybir

F32 = mybir.dt.float32
F32R = mybir.dt.float32r
ALU = mybir.AluOpType
ACT = mybir.ActivationFunctionType
AX = mybir.AxisListType

B, T, D, KV = 16, 100, 512, 722
DH, NH, NBR = 32, 16, 4
CC = D // 128
BRANCHES = [(16, 0), (128, 16), (128, 0), (256, 144)]
LIVE = [br for br, (high, low) in enumerate(BRANCHES) if low < T]
NL = len(LIVE)
assert LIVE == list(range(NL)) and NL == NBR - 1
TOPK = 32
SCALE = DH ** -0.5
LN_EPS = 1e-5
RMS_EPS = float(np.finfo(np.float32).eps)
REMOVED = -3.0e38


class At:

    def __init__(self, const, reg=None, factor=1):
        self.const, self.reg, self.factor = const, reg, factor

    def next(self, n=1):
        return At(self.const + n, self.reg, self.factor)

    def count(self, per, k):
        n = self.const * per + k
        return n if self.reg is None else self.reg * (self.factor * per) + n


def need(eng, sem, value):
    if not isinstance(value, int) or value > 0:
        eng.wait_ge(sem, value)


def settle(eng):
    eng.nop(nofuse=True)


class Order:

    def __init__(self, eng, sem):
        self.eng, self.sem, self.n = eng, sem, 0

    def mark(self, ins):
        ins.then_inc(self.sem, 1)
        self.n += 1
        return self.n

    def after(self, n):
        self.eng.wait_ge(self.sem, n)

    def finish(self):
        if self.n:
            self.eng.wait_ge(self.sem, self.n)
            self.eng.sem_clear(self.sem)
        self.n = 0


def split3(pe, out, ah, al, bh, bl, start, stop):
    pe.matmul(out, ah, bh, start=start, stop=False)
    pe.matmul(out, ah, bl, start=False, stop=False)
    return pe.matmul(out, al, bh, start=False, stop=stop)


def row_stats(dve, order, x, stats, mv, done):
    order.after(order.mark(dve.bn_stats(stats, x)))
    order.after(order.mark(dve.bn_aggr(mv, stats)))
    dve.tensor_scalar(mv[:, 1:2], mv[:, 1:2], LN_EPS, None, ALU.add).then_inc(done, 1)


def spectral_program(nc, A, M):
    FOLDS = ("pp", "mp", "pm", "mm")
    even, pairs, odd = slice(0, D // 2 + 1), slice(1, D // 2), slice(D // 2 + 1, D)
    with ExitStack() as ctx:
        sb = lambda n, s, d=F32: ctx.enter_context(nc.sbuf_tensor("sp_" + n, s, d))
        sem = lambda n: ctx.enter_context(nc.semaphore("sp_" + n))
        W = {n: sb("W" + n, [128, CC, D]) for n in FOLDS}
        Y = W["pp"]
        G, X = sb("G", [128, CC, D]), sb("X", [128, CC, D])
        signs = sb("signs", [128, CC, 4, 2])
        acc = ctx.enter_context(nc.psum_tensor("sp_acc", [128, 2 * CC, 512], F32))
        signs_in, order_sem = sem("signs_in"), sem("order")
        loaded = [sem(f"loaded{c}") for c in range(CC)]
        folded, x_mm, x_ready, m_mm, m_ready = (sem(n) for n in ("folded", "x_mm", "x_ready", "m_mm", "m_ready"))
        block = ctx.enter_context(nc.Block())

        @block.sync
        def _(sp):
            sp.dma_start(signs[:, :, :, :], A["fold_signs"]).then_inc(signs_in, 16)
            for c in range(CC):
                rows = slice(128 * c, 128 * c + 128)
                for n in FOLDS:
                    sp.dma_start(W[n][:, c, :], A["W" + n][rows, :]).then_inc(loaded[c], 16)
                sp.dma_start(G[:, c, :], A["dft"][rows, :]).then_inc(loaded[c], 16)

        @block.vector
        def _(dve):
            order = Order(dve, order_sem)
            dve.wait_ge(signs_in, 16)
            for c in range(CC):
                dve.wait_ge(loaded[c], 16 * (len(FOLDS) + 1))
                done = {0: order.mark(dve.tensor_scalar(Y[:, c, even], Y[:, c, even], signs[:, c, 0, 0:1], None,
                                                        ALU.mult))}
                for f in (1, 2, 3):
                    for kind in range(2):
                        cols = odd if kind else (even if FOLDS[f] == "pm" else pairs)
                        if kind in done:
                            order.after(done[kind])
                        done[kind] = order.mark(dve.scalar_tensor_tensor(
                            Y[:, c, cols], W[FOLDS[f]][:, c, cols], signs[:, c, f, kind:kind + 1], Y[:, c, cols],
                            ALU.mult, ALU.add))
                order.after(order.n)
                dve.sem_inc(folded, 1)

        @block.tensor
        def _(pe):
            for c in range(CC):
                pe.wait_ge(folded, c + 1)
                for k in range(CC):
                    last = pe.matmul(acc[:, k, :], Y[:, c, 128 * k:128 * k + 128], G[:, c, :],
                                     start=c == 0, stop=c == CC - 1)
                    if c == CC - 1:
                        last.then_inc(x_mm, 1)
            for c in range(CC):
                pe.wait_ge(x_ready, c + 1)
                for k in range(CC):
                    last = pe.matmul(acc[:, CC + k, :], G[:, c, 128 * k:128 * k + 128], X[:, c, :],
                                     start=c == 0, stop=c == CC - 1)
                    if c == CC - 1:
                        last.then_inc(m_mm, 1)

        @block.scalar
        def _(act):
            for c in range(CC):
                act.wait_ge(x_mm, c + 1)
                act.activation(X[:, c, :], acc[:, c, :], ACT.Copy).then_inc(x_ready, 1)
            for c in range(CC):
                act.wait_ge(m_mm, c + 1)
                act.activation(M[:, c, :], acc[:, CC + c, :], ACT.Copy, scale=1.0 / D).then_inc(m_ready, 1)


def self_program(nc, A, x1_dram):
    NQ = NL * D
    NQK = NQ + D
    QB = NQK // D
    HEADS = NQK // DH
    QC = NQK // 128
    HK = 4
    PV = HK * NL * (DH + 1)
    RING = NH * NL * T // D
    SV = 2
    with ExitStack() as ctx:
        sb = lambda n, s, d=F32: ctx.enter_context(nc.sbuf_tensor("sa_" + n, s, d))
        ps = lambda n, s: ctx.enter_context(nc.psum_tensor("sa_" + n, s, F32))
        sem = lambda n: ctx.enter_context(nc.semaphore("sa_" + n))
        heads = lambda t, n: t.rearrange("p (h d) -> p h d", h=n)
        WqkH, WqkL = sb("WqkH", [128, CC, NQK], F32R), sb("WqkL", [128, CC, NQK], F32R)
        WvH, WvL = sb("WvH", [128, CC, SV * D], F32R), sb("WvL", [128, CC, SV * D], F32R)
        Wv, WO = sb("Wv", [128, CC, (NBR - SV) * D]), sb("WO", [128, CC, D])
        ident = sb("ident", [128, 128])
        cos, sin = sb("cos", [T, DH // 2]), sb("sin", [T, DH // 2])
        bias_qk, bias_o = sb("bias_qk", [T, NQK]), sb("bias_o", [T, D])
        bv3, vn3, es3, k3, r3, cb = (sb(n, [128, CC]) for n in ("bv3", "vn3", "es3", "k3", "r3", "cb"))
        bvl = sb("bvl", [128, NL, CC])
        xin, xn, xres, x1 = (sb(n, [T, D]) for n in ("xin", "xn", "xres", "x1"))
        stats, mv, rstd = sb("stats", [T, 6]), sb("mv", [T, 2]), sb("rstd", [T, 1])
        xT = sb("xT", [128, CC, T])
        xTh, xTl = sb("xTh", [128, CC, T], F32R), sb("xTl", [128, CC, T], F32R)
        xsum, out3 = sb("xsum", [128, CC]), sb("out3", [128, CC])
        qk, rq, ss = sb("qk", [T, NQK]), sb("rq", [T, NQK]), sb("ss", [T, HEADS])
        minus_half, step = sb("minus_half", [T, HEADS]), sb("step", [1, 1])
        tmp = sb("tmp", [T, NQ])
        qkTh, qkTl = sb("qkTh", [128, QC, T], F32R), sb("qkTl", [128, QC, T], F32R)
        E = sb("E", [128, NH, NL, T])
        V = sb("V", [T + 1, NH, NL, DH + 1])
        rden = sb("rden", [T, NH * NL])
        ctxr, ctxT = sb("ctxr", [T, D]), sb("ctxT", [128, CC, T])
        pp, pq = ps("pp", [128, 2, 512]), ps("pq", [128, 4, 512])
        pt, pw = ps("pt", [128, 512]), ps("pw", [128, 512])

        x_in, xres_in, x1_out = sem("x_in"), sem("xres_in"), sem("x1_out")
        setup_in, null_in = sem("setup_in"), sem("null_in")
        dve_order, pool_order = sem("dve_order"), sem("pool_order")
        staged = [sem(f"staged{r}") for r in range(RING)]
        hi_made, lo_made = sem("hi_made"), sem("lo_made")
        sink_steps, null_weights, null_values = sem("sink_steps"), sem("null_weights"), sem("null_values")
        xn_ready, xres_ready = sem("xn_ready"), sem("xres_ready")
        var_ready, rstd_ready, ss_ready, norm_ready = (sem(n) for n in ("var_ready", "rstd_ready", "ss_ready", "norm_ready"))
        xT_mm, xT_hi, xT_copy, xT_lo, sum_ready = (sem(n) for n in ("xT_mm", "xT_hi", "xT_copy", "xT_lo", "sum_ready"))
        v3_mm, out3_ready = sem("v3_mm"), sem("out3_ready")
        qk_mm, qk_ready, sq_ready, roped = sem("qk_mm"), sem("qk_ready"), sem("sq_ready"), sem("roped")
        v_mm, v_ready = sem("v_mm"), sem("v_ready")
        hT_mm, hT_hi, hT_lo = sem("hT_mm"), sem("hT_hi"), sem("hT_lo")
        s_mm, e_ready, masked = sem("s_mm"), sem("e_ready"), sem("masked")
        pv_mm, pv_used, ctx_ready = sem("pv_mm"), sem("pv_used"), sem("ctx_ready")
        cT_mm, cT_ready, y_mm, x1_ready = sem("cT_mm"), sem("cT_ready"), sem("y_mm"), sem("x1_ready")

        piece = lambda n: slice(D * n, D * n + D)
        UNITS = [(A["WQ"] if n < NL else A["WK"], piece(n if n < NL else 0), WqkH, WqkL, c, piece(n))
                 for c in range(CC) for n in range(QB)]
        UNITS += [(A["WV"], piece(n), WvH, WvL, c, piece(n)) for c in range(CC) for n in range(SV)]
        stage = [E[:, :, :, :].rearrange("p h n q -> p (h n q)")[:, piece(u)] for u in range(RING)]
        sinks0, tanh0, exp0 = (qk[0:1, 64 * n:64 * n + NH * NL] for n in range(3))
        SETUP = [
            (WO[:, :, :], A["WO"].rearrange("(c p) o -> p c o", p=128)),
            (ident[:, :], A["ident"]), (cos[:, :], A["cos"]), (sin[:, :], A["sin"]),
            (bias_qk[:, 0:NQ], A["bQ"][0:1, 0:NQ].broadcast_to((T, NQ))),
            (bias_qk[:, NQ:NQK], A["bK"][0:1, :].broadcast_to((T, D))),
            (bias_o[:, :], A["bO"][0:1, :].broadcast_to((T, D))),
            (bv3[:, :], A["bV_cols"][:, NL * CC:]),
            (vn3[:, :], A["v_nulls_cols"][:, NL * CC:]),
            (es3[:, :], A["sinks_cols"][:, NL * CC:]),
            (sinks0, A["sinks"][0:1, 0:NL * NH]),
            (rq[0:1, 0:NQ], A["v_nulls"][0:1, 0:NQ]),
            (tmp[0:1, 0:NQ], A["bV"][0:1, 0:NQ]),
        ]
        SETUP += [(bvl[:, n, :], A["bV_cols"][:, CC * n:CC * n + CC]) for n in range(NL)]
        SETUP += [(Wv[:, c, :], A["WV"][128 * c:128 * c + 128, SV * D:]) for c in range(CC)]

        v_bank, qk_bank = (lambda br: br % 2), (lambda n: (n + 1) % 2)

        block = ctx.enter_context(nc.Block())

        def each_batch(eng, body):
            body(At(-1), cur=False, prev=False, nxt=True)
            body(At(0), cur=True, prev=False, nxt=True)
            body(At(1), cur=True, prev=True, nxt=True)
            with eng.Fori(2, B - 1) as i:
                body(At(0, i), cur=True, prev=True, nxt=True)
            body(At(B - 1), cur=True, prev=True, nxt=False)
            body(At(B), cur=False, prev=True, nxt=False)

        def batch_of(dram, b, n):
            i = b.const + n if b.reg is None else b.reg + (b.const + n)
            return dram[bass.ds(i, 1)].rearrange("o t d -> (o t) d")

        @block.sync
        def _(sp):
            for u, (w, cols, _, _, c, _) in enumerate(UNITS):
                if u >= RING:
                    sp.wait_ge(hi_made, u - RING + 1)
                    sp.wait_ge(lo_made, u - RING + 1)
                sp.dma_start(stage[u % RING], w[128 * c:128 * c + 128, cols]).then_inc(staged[u % RING], 16)

            def body(b, cur, prev, nxt):
                if nxt:
                    need(sp, xn_ready, b.count(1, 1))
                    sp.dma_start(xin[:, :], batch_of(A["x"], b, 1)).then_inc(x_in, 16)
                if prev:
                    need(sp, x1_ready, b.count(1, -1))
                    sp.dma_start(xres[:, :], batch_of(A["x"], b, -1)).then_inc(xres_in, 16)
                    sp.wait_ge(x1_ready, b.count(1, 0))
                    sp.dma_start(batch_of(x1_dram, b, -1), x1[:, :]).then_inc(x1_out, 16)
            each_batch(sp, body)
            sp.wait_ge(x1_out, 16 * B)

        @block.gpsimd
        def _(pool):
            for t, a in SETUP:
                pool.dma_start(t, a).then_inc(setup_in, 16)
            pool.wait_ge(null_weights, 1)
            pool.dma_start(E[T:T + 1, :, :, :].rearrange("p h n q -> p (h n q)"),
                           E[0:1, :, :, :].rearrange("p h n q -> p (h n q)")).then_inc(null_in, 16)
            pool.wait_ge(null_values, 1)
            pool.dma_start(V[T:T + 1, :, :, :].rearrange("p h n d -> p (h n d)"),
                           V[0:1, :, :, :].rearrange("p h n d -> p (h n d)")).then_inc(null_in, 16)
            order = Order(pool, pool_order)
            order.mark(pool.memset(minus_half[:, :], -0.5))
            order.finish()
            one = pool.to_reg(1.0)

            def body(b, cur, prev, nxt):
                bn = b.next()
                if nxt:
                    pool.wait_ge(var_ready, bn.count(1, 1))
                    pool.tensor_tensor(rstd[:, :], mv[:, 1:2], minus_half[:, 0:1], ALU.pow).then_inc(rstd_ready, 1)
                if prev:
                    pool.wait_ge(xres_in, b.count(16, 0))
                    pool.tensor_tensor(xres[:, :], xres[:, :], bias_o[:, :], ALU.add).then_inc(xres_ready, 1)
                for g in range(QB + 1):
                    if cur and g < NH // 4:
                        pool.wait_ge(e_ready, b.count(NH, 4 * g + 4))
                        order.mark(pool.tensor_tensor(step[:, :], minus_half[0:1, 0:1], minus_half[0:1, 0:1], ALU.mult))
                        for br in LIVE:
                            high, low = BRANCHES[br]
                            part = E[0:T, 4 * g:4 * g + 4, br, :]
                            windows = [(-low, 1)] + ([(high - 1, -1)] if high < T else [])
                            for base, sign in windows:
                                order.after(order.n)
                                ins = pool.affine_select(
                                    out=part, in_=part, compare_op=ALU.is_ge, fill=one, base=base,
                                    pattern=[[0, 4], [sign, T]], channel_multiplier=-sign)
                                if (g, br, sign) == (NH // 4 - 1, LIVE[-1], windows[-1][1]):
                                    ins.then_inc(masked, 1)
                                else:
                                    order.mark(ins)
                    if nxt and g:
                        part = ss[:, NH * (g - 1):NH * g]
                        pool.wait_ge(ss_ready, bn.count(QB, g))
                        pool.tensor_tensor(part, part, minus_half[:, 0:NH], ALU.pow).then_inc(norm_ready, 1)
                order.finish()
            each_batch(pool, body)

        @block.scalar
        def _(act):
            for u, (_, _, high, _, c, to) in enumerate(UNITS):
                act.wait_ge(staged[u % RING], 16 * (u // RING + 1))
                act.activation(high[:, c, to], stage[u % RING], ACT.Copy).then_inc(hi_made, 1)
            act.wait_ge(setup_in, 16 * len(SETUP))
            act.activation(tanh0, sinks0, ACT.Tanh).then_inc(sink_steps, 1)
            act.activation(r3[:, :], es3[:, :], ACT.Tanh).then_inc(sink_steps, 1)
            act.wait_ge(sink_steps, 2)
            act.activation(exp0, tanh0, ACT.Exp).then_inc(sink_steps, 1)
            act.activation(es3[:, :], r3[:, :], ACT.Exp).then_inc(sink_steps, 1)
            act.wait_ge(sink_steps, 4)
            act.wait_ge(lo_made, len(UNITS))
            for br in range(NL):
                w = exp0[:, NH * br:NH * br + NH].unsqueeze(2).broadcast_to((1, NH, T))
                last = act.activation(E[0:1, :, br, :], w, ACT.Copy)
            last.then_inc(null_weights, 1)

            def body(b, cur, prev, nxt):
                bn = b.next()
                if cur:
                    need(act, pv_mm, b.count(1, 0))
                    if not prev:
                        act.wait_ge(null_in, 32)
                    for br in range(NL):
                        act.wait_ge(v_mm, b.count(NL, br + 1))
                        act.activation(V[0:T, :, br, 0:DH], heads(pp[0:T, v_bank(br), :], NH),
                                       ACT.Copy).then_inc(v_ready, 1)
                    for g in range(QC // 4):
                        act.wait_ge(hT_mm, b.count(QC // 4, g + 1))
                        act.activation(qkTh[:, 4 * g:4 * g + 4, :], heads(pp[:, qk_bank(g), 0:4 * T], 4),
                                       ACT.Copy).then_inc(hT_hi, 1)
                if nxt:
                    act.wait_ge(xT_mm, bn.count(1, 1))
                    act.activation(xTh[:, :, :], heads(pt[:, 0:CC * T], CC), ACT.Copy).then_inc(xT_hi, 1)
                for g in range(QB + 1):
                    if cur and g < NH // 4:
                        for h in range(4 * g, 4 * g + 4):
                            act.wait_ge(s_mm, b.count(NH, h + 1))
                            act.activation(E[0:T, h, :, :], heads(pq[0:T, h % 4, 0:NL * T], NL), ACT.Exp).then_inc(e_ready, 1)
                    if nxt and g:
                        n = g - 1
                        if n == 0:
                            need(act, hT_mm, bn.count(QC // 4, 0))
                        act.wait_ge(qk_ready, bn.count(QB, g))
                        act.activation(rq[:, D * n:D * n + D], qk[:, D * n:D * n + D], ACT.Square).then_inc(sq_ready, 1)
            each_batch(act, body)

        @block.vector
        def _(dve):
            for u, (_, _, high, low, c, to) in enumerate(UNITS):
                dve.wait_ge(hi_made, u + 1)
                dve.tensor_tensor(low[:, c, to], stage[u % RING], high[:, c, to].bitcast(F32),
                                  ALU.subtract).then_inc(lo_made, 1)
            order = Order(dve, dve_order)
            then = lambda ins: order.after(order.mark(ins))
            dve.wait_ge(setup_in, 16 * len(SETUP))
            then(dve.memset(V[:, :, :, :], 1.0))
            for br in range(NL):
                last = dve.tensor_tensor(V[0:1, :, br, 0:DH], heads(rq[0:1, D * br:D * br + D], NH),
                                         heads(tmp[0:1, D * br:D * br + D], NH), ALU.subtract)
                if br < NL - 1:
                    order.mark(last)
            order.after(order.n)
            last.then_inc(null_values, 1)
            then(dve.tensor_tensor(cb[:, :], bvl[:, 0, :], bvl[:, 1, :], ALU.add))
            then(dve.tensor_tensor(cb[:, :], cb[:, :], bvl[:, 2, :], ALU.add))
            then(dve.tensor_scalar(cb[:, :], cb[:, :], 1.0 / NBR, None, ALU.mult))
            dve.wait_ge(sink_steps, 4)
            then(dve.tensor_tensor(k3[:, :], es3[:, :], vn3[:, :], ALU.mult))
            then(dve.scalar_tensor_tensor(k3[:, :], bv3[:, :], float(T), k3[:, :], ALU.mult, ALU.add))
            then(dve.tensor_scalar(r3[:, :], es3[:, :], float(T), float(NBR), ALU.add, ALU.mult))
            then(dve.reciprocal(r3[:, :], r3[:, :]))
            order.finish()

            half = DH // 2
            qk3, rq3 = heads(qk[:, :], HEADS), heads(rq[:, :], HEADS)
            even, odd = qk3[:, :, 0:DH:2], qk3[:, :, 1:DH:2]
            first, second = rq3[:, :, 0:half], rq3[:, :, half:DH]
            t3 = heads(tmp[:, 0:HEADS * half], HEADS)
            cos3, sin3 = (t[:, :].unsqueeze(1).broadcast_to((T, HEADS, DH // 2)) for t in (cos, sin))
            def body(b, cur, prev, nxt):
                bn = b.next()
                if nxt:
                    dve.wait_ge(x_in, bn.count(16, 16))
                    row_stats(dve, order, xin[:, :], stats[:, :], mv[:, :], var_ready)
                if prev:
                    dve.wait_ge(cT_mm, b.count(1, 0))
                    dve.wait_ge(out3_ready, b.count(1, 0))
                    dve.tensor_tensor(ctxT[:, :, :], heads(pt[:, 0:CC * T], CC),
                                      out3[:, :].unsqueeze(2).broadcast_to((128, CC, T)), ALU.add).then_inc(cT_ready, 1)
                if nxt:
                    need(dve, xT_mm, b.count(1, 1))
                    dve.wait_ge(rstd_ready, bn.count(1, 1))
                    dve.tensor_scalar(xn[:, :], xin[:, :], mv[:, 0:1], rstd[:, :],
                                      ALU.subtract, ALU.mult).then_inc(xn_ready, 1)
                if cur:
                    for g in range(QC // 4):
                        dve.wait_ge(hT_hi, b.count(QC // 4, g + 1))
                        dve.tensor_tensor(qkTl[:, 4 * g:4 * g + 4, :], heads(pp[:, qk_bank(g), 0:4 * T], 4),
                                          qkTh[:, 4 * g:4 * g + 4, :].bitcast(F32), ALU.subtract).then_inc(hT_lo, 1)
                if prev:
                    need(dve, x1_out, b.count(16, -16))
                    dve.wait_ge(xres_ready, b.count(1, 0))
                    dve.wait_ge(y_mm, b.count(1, 0))
                    dve.tensor_tensor(x1[:, :], pw[0:T, :], xres[:, :], ALU.add).then_inc(x1_ready, 1)
                if nxt:
                    dve.wait_ge(xT_hi, bn.count(1, 1))
                    dve.tensor_copy(xT[:, :, :], heads(pt[:, 0:CC * T], CC)).then_inc(xT_copy, 1)
                    dve.wait_ge(xT_copy, bn.count(1, 1))
                    dve.tensor_tensor(xTl[:, :, :], xT[:, :, :], xTh[:, :, :].bitcast(F32), ALU.subtract).then_inc(xT_lo, 1)
                    for n in range(QB + 1):
                        if n < QB:
                            dve.wait_ge(qk_mm, bn.count(QB, n + 1))
                            dve.tensor_tensor(qk[:, D * n:D * n + D], pp[0:T, qk_bank(n), :],
                                              bias_qk[:, D * n:D * n + D], ALU.add).then_inc(qk_ready, 1)
                        if n:
                            part = ss[:, NH * (n - 1):NH * n]
                            dve.wait_ge(sq_ready, bn.count(QB, n))
                            ins = dve.tensor_reduce(part, rq3[:, NH * (n - 1):NH * n, :], AX.X, ALU.add)
                            if n <= NL:
                                then(ins)
                                ins = dve.tensor_scalar(part, part, 1.0 / DH, RMS_EPS, ALU.mult, ALU.add)
                            ins.then_inc(ss_ready, 1)
                    need(dve, v3_mm, b.count(1, 1))
                    dve.tensor_reduce(xsum[:, :], xT[:, :, :], AX.X, ALU.add).then_inc(sum_ready, 1)
                    dve.wait_ge(norm_ready, bn.count(QB, QB))
                    then(dve.tensor_tensor(qk3, qk3, ss[:, :].unsqueeze(2).broadcast_to((T, HEADS, DH)), ALU.mult))
                    order.mark(dve.tensor_tensor(t3, odd, sin3, ALU.mult))
                    order.mark(dve.tensor_tensor(first, even, cos3, ALU.mult))
                    then(dve.tensor_tensor(second, even, sin3, ALU.mult))
                    then(dve.tensor_tensor(first, first, t3, ALU.subtract))
                    then(dve.tensor_tensor(t3, odd, cos3, ALU.mult))
                    dve.tensor_tensor(second, second, t3, ALU.add).then_inc(roped, 1)
                if cur:
                    dve.wait_ge(v3_mm, b.count(1, 1))
                    then(dve.tensor_tensor(out3[:, :], pw[:, 0:CC], k3[:, :], ALU.add))
                    then(dve.tensor_tensor(out3[:, :], out3[:, :], r3[:, :], ALU.mult))
                    dve.tensor_tensor(out3[:, :], out3[:, :], cb[:, :], ALU.add).then_inc(out3_ready, 1)
                    dve.wait_ge(roped, b.count(1, 1))
                    dve.wait_ge(pv_mm, b.count(1, 1))
                    pv = pq[0:T, :, 0:PV].rearrange("p k (n d) -> p k n d", d=DH + 1)
                    then(dve.tensor_scalar(rden[:, :].rearrange("p (k n) -> p k n", k=4), pv[:, :, :, DH],
                                           float(NBR), None, ALU.mult))
                    then(dve.reciprocal(rden[:, :], rden[:, :]))
                    t4 = tmp[:, :].rearrange("p (k n d) -> p k n d", k=4, d=DH)
                    n4 = HK * NL
                    for k in range(4):
                        ins = dve.tensor_tensor(t4[:, k], pv[:, k, :, 0:DH],
                                                rden[:, n4 * k:n4 * k + n4].unsqueeze(2).broadcast_to((T, n4, DH)), ALU.mult)
                        ins.then_inc(pv_used, 1)
                    dve.wait_ge(pv_used, b.count(4, 4))
                    t5 = tmp[:, :].rearrange("p (h n d) -> p n h d", h=NH, n=NL)
                    c3 = heads(ctxr[:, :], NH)
                    then(dve.tensor_tensor(c3, t5[:, 0], t5[:, 1], ALU.add))
                    dve.tensor_tensor(c3, c3, t5[:, 2], ALU.add).then_inc(ctx_ready, 1)
                order.finish()
            each_batch(dve, body)

        @block.tensor
        def _(pe):
            pe.wait_ge(lo_made, CC * QB)

            def body(b, cur, prev, nxt):
                bn = b.next()
                for br in range(NL):
                    if cur:
                        if br < 2:
                            pe.wait_ge(qk_ready, b.count(QB, QB - br))
                        else:
                            pe.wait_ge(v_ready, b.count(NL, br - 1))
                        if not prev and br == 0:
                            pe.wait_ge(lo_made, len(UNITS))
                        for c in range(CC):
                            if br < SV:
                                last = split3(pe, pp[0:T, v_bank(br), :], xTh[:, c, :], xTl[:, c, :],
                                              WvH[:, c, piece(br)], WvL[:, c, piece(br)], c == 0, c == CC - 1)
                            else:
                                last = pe.matmul(pp[0:T, v_bank(br), :], xT[:, c, :], Wv[:, c, piece(br - SV)],
                                                 start=c == 0, stop=c == CC - 1)
                        last.then_inc(v_mm, 1)
                    if br == 1 and prev:
                        pe.wait_ge(ctx_ready, b.count(1, 0))
                        for c in range(CC):
                            last = pe.transpose(pt[:, T * c:T * c + T], ctxr[:, 128 * c:128 * c + 128], ident[0:T, 0:T])
                        last.then_inc(cT_mm, 1)
                if cur:
                    pe.wait_ge(roped, b.count(1, 1))
                    for g in range(QC // 4):
                        if g < 2:
                            pe.wait_ge(v_ready, b.count(NL, 2 + g))
                        else:
                            pe.wait_ge(hT_lo, b.count(QC // 4, g - 1))
                        for i in range(4):
                            last = pe.transpose(pp[:, qk_bank(g), T * i:T * i + T],
                                                rq[:, 128 * (4 * g + i):128 * (4 * g + i) + 128], ident[0:T, 0:T])
                        last.then_inc(hT_mm, 1)
                if prev:
                    pe.wait_ge(cT_ready, b.count(1, 0))
                    for c in range(CC):
                        last = pe.matmul(pw[0:T, :], ctxT[:, c, :], WO[:, c, :], start=c == 0, stop=c == CC - 1)
                    last.then_inc(y_mm, 1)
                if nxt:
                    pe.wait_ge(xn_ready, bn.count(1, 1))
                    need(pe, cT_ready, b.count(1, 0))
                    for c in range(CC):
                        last = pe.transpose(pt[:, T * c:T * c + T], xn[:, 128 * c:128 * c + 128], ident[0:T, 0:T])
                    last.then_inc(xT_mm, 1)
                if cur:
                    pe.wait_ge(hT_lo, b.count(QC // 4, QC // 4))
                for n in range(QB):
                    if cur:
                        for h in range(4 * n, 4 * n + 4):
                            if h < 4:
                                need(pe, pv_used, b.count(4, 0))
                            else:
                                pe.wait_ge(e_ready, b.count(NH, h - 3))
                            rows, g = slice(DH * (h % 4), DH * (h % 4) + DH), h // 4
                            q = lambda t: t[rows, g:NL * 4:4, :]
                            k = lambda t: t[rows, NL * 4 + g, :]
                            split3(pe, heads(pq[0:T, h % 4, 0:NL * T], NL), k(qkTh), k(qkTl), q(qkTh), q(qkTl),
                                   True, True).then_inc(s_mm, 1)
                    if nxt:
                        if n == 0:
                            pe.wait_ge(xT_lo, bn.count(1, 1))
                        if n < 2:
                            need(pe, hT_lo, b.count(QC // 4, 3 + n))
                        else:
                            pe.wait_ge(qk_ready, bn.count(QB, n - 1))
                        cols = slice(D * n, D * n + D)
                        for c in range(CC):
                            last = split3(pe, pp[0:T, qk_bank(n), :], xTh[:, c, :], xTl[:, c, :],
                                          WqkH[:, c, cols], WqkL[:, c, cols], c == 0, c == CC - 1)
                        last.then_inc(qk_mm, 1)
                if cur:
                    pe.wait_ge(sum_ready, b.count(1, 1))
                    need(pe, x1_ready, b.count(1, 0))
                    for o in range(CC):
                        for c in range(CC):
                            last = pe.matmul(pw[:, o:o + 1], Wv[:, c, NQ - SV * D + 128 * o:NQ - SV * D + 128 * o + 128],
                                             xsum[:, c:c + 1], start=c == 0, stop=c == CC - 1)
                    last.then_inc(v3_mm, 1)
                if cur:
                    pe.wait_ge(v_ready, b.count(NL, NL))
                    pe.wait_ge(masked, b.count(1, 1))
                    if not prev:
                        pe.wait_ge(null_in, 32)
                    for h in range(NH):
                        for br in range(NL):
                            at = ((h % HK) * NL + br) * (DH + 1)
                            last = pe.matmul(pq[0:T, h // HK, at:at + DH + 1], E[0:T + 1, h, br, :], V[:, h, br, :],
                                             start=True, stop=True)
                    last.then_inc(pv_mm, 1)
            each_batch(pe, body)


class Tile:

    REST = 4 * T - 3 * 128

    def __init__(self, i):
        self.i = i
        self.rest = i == 12
        self.g, self.t = divmod(i, 3)
        self.rows = 4 * self.REST if self.rest else 128
        self.dims = 128 if self.rest else 2 * DH

    def blocks(self):
        if self.rest:
            return [(DH * g, slice(self.REST * g, self.REST * (g + 1)), 3 * DH, g, slice(T - self.REST, T))
                    for g in range(4)]
        out = []
        for n in range(2):
            h = self.t + n
            lo, hi = max(128 * self.t, T * h), min(128 * self.t + 128, T * h + T)
            out.append((DH * n, slice(lo - 128 * self.t, hi - 128 * self.t), DH * h, self.g, slice(lo - T * h, hi - T * h)))
        return out


def cross_program(nc, A, M, x1_dram, out_dram):
    NT = 13
    STEPS = [[Tile(i) for i in range(NT)][2 * s:2 * s + 2] for s in range(7)]
    KC = 6
    HALF = 3 * 128
    HALVES = [(0, HALF), (HALF, KV - HALF)]
    KEY0 = [128 * k for k in range(KC - 1)] + [KV - 128]
    SPLIT = 150
    RING = 4
    SLICES = [(half, kind, n) for half in range(2) for kind, n in
              [("K", g) for g in range(4)] + [("V", 3 * half + k) for k in range(3)]]
    NSL = len(SLICES)
    PLAN = [([12, 13], []), ([], [0, 1]), ([2], [3]), ([4, 5], [6]), ([], [7, 8]), ([9], [10]), ([11], [])]
    assert [n for a, b in PLAN[1:] + PLAN[:1] for n in a + b] == list(range(NSL))
    with ExitStack() as ctx:
        sb = lambda n, s, d=F32: ctx.enter_context(nc.sbuf_tensor("ca_" + n, s, d))
        ps = lambda n, s: ctx.enter_context(nc.psum_tensor("ca_" + n, s, F32))
        sem = lambda n: ctx.enter_context(nc.semaphore("ca_" + n))
        chunks = lambda t, n: t.rearrange("p (c d) -> p c d", c=n)
        WkH, WkL, WvH, WvL = (sb(n, [128, CC, D], F32R) for n in ("WkH", "WkL", "WvH", "WvL"))
        WqT, WoT = sb("WqT", [128, CC, D]), sb("WoT", [128, CC, D])
        ident = sb("ident", [128, 128])
        tail_keys = sb("tail_keys", [128, 1])
        bq, bk, bv = (sb(n, [128, CC]) for n in ("bq", "bk", "bv"))
        bias_o, bias_f = sb("bias_o", [T, D]), sb("bias_f", [T, D])
        minus_half = sb("minus_half", [T, 1])
        raw = sb("raw", [128, 2, HALF])
        cH, cL = sb("cH", [128, CC, HALF], F32R), sb("cL", [128, CC, HALF], F32R)
        K32 = sb("K32", [128, HALF])
        KH = [sb(f"KH{p}", [128, CC, KV], F32R) for p in range(2)]
        KL = [sb(f"KL{p}", [128, CC, KV], F32R) for p in range(2)]
        V = [sb(f"V{p}", [128, KC, D]) for p in range(2)]
        QH, QL = sb("QH", [128, CC, 4 * T], F32R), sb("QL", [128, CC, 4 * T], F32R)
        REST = Tile.REST
        RH, RL = (sb(n, [128, 5 * 4 * REST], F32R) for n in ("RH", "RL"))
        S = [sb(f"S{r}", [128, KV]) for r in range(RING)]
        E = [sb(f"E{r}", [128, KV]) for r in range(RING)]
        W = [sb(f"W{r}", [128, KV]) for r in range(2)]
        top = [sb(f"top{r}", [128, TOPK]) for r in range(RING)]
        shift, Z, rZ = (sb(n, [128, RING]) for n in ("shift", "Z", "rZ"))
        PT = sb("PT", [128, KC, 128])
        On = sb("On", [128, 128])
        ctxT = sb("ctxT", [128, CC, T])
        xin, xn, x2 = (sb(n, [T, D]) for n in ("xin", "xn", "x2"))
        xb = [sb(f"xb{p}", [T, D]) for p in range(2)]
        stats, mv, rstd = sb("stats", [T, 6]), sb("mv", [T, 2]), sb("rstd", [T, 1])
        xT = sb("xT", [128, CC, T])
        pS, pT = ps("pS", [128, 1024]), ps("pT", [128, 1024])
        pO, pF, pX = ps("pO", [128, 512]), ps("pF", [128, 2, 512]), ps("pX", [128, 512])
        scores = pS[:, SPLIT:SPLIT + KV]

        setup_in, w_in, w_hi, w_lo = sem("setup_in"), sem("w_in"), sem("w_hi"), sem("w_lo")
        zeroed, bias_mm, bias_ready = sem("zeroed"), sem("bias_mm"), sem("bias_ready")
        dve_order, pool_order = sem("dve_order"), sem("pool_order")
        ctx_in, x_in, x2_free = sem("ctx_in"), sem("x_in"), sem("x2_free")
        ctx_hi, ctx_lo = sem("ctx_hi"), sem("ctx_lo")
        kv_mm, kv_out, k_hi, k_lo = sem("kv_mm"), sem("kv_out"), sem("k_hi"), sem("k_lo")
        var1_ready, rstd1_ready, xn1_ready, x1T_mm, x1T_ready = (
            sem(n) for n in ("var1_ready", "rstd1_ready", "xn1_ready", "x1T_mm", "x1T_ready"))
        var2_ready, rstd2_ready, xn2_ready, x2T_mm, x2T_ready = (
            sem(n) for n in ("var2_ready", "rstd2_ready", "xn2_ready", "x2T_mm", "x2T_ready"))
        xb_ready = sem("xb_ready")
        q_mm, q_ready, q_hi, q_lo = sem("q_mm"), sem("q_ready"), sem("q_hi"), sem("q_lo")
        s_mm, s_ready, shift_ready, e_ready = sem("s_mm"), sem("s_ready"), sem("shift_ready"), sem("e_ready")
        picked, f_ready, z_ready, rz_ready, p_ready = (sem(n) for n in ("picked", "f_ready", "z_ready", "rz_ready", "p_ready"))
        pt_mm, pt_ready, o_mm, o_ready, ot_mm, ot_ready = (
            sem(n) for n in ("pt_mm", "pt_ready", "o_mm", "o_ready", "ot_mm", "ot_ready"))
        y_mm, x2_ready, x2f_ready, f_mm, out_ready = (sem(n) for n in ("y_mm", "x2_ready", "x2f_ready", "f_mm", "out_ready"))

        SETUP = [(WqT[:, :, :], A["WqT"].rearrange("(c p) o -> p c o", p=128)),
                 (WoT[:, :, :], A["WoT"].rearrange("(c p) o -> p c o", p=128)),
                 (ident[:, :], A["ident"]), (tail_keys[:, :], A["tail_keys"]),
                 (bq[:, :], A["xbq"]), (bk[:, :], A["xbk"]), (bv[:, :], A["xbv"]),
                 (bias_o[:, :], A["xbo"][0:1, :].broadcast_to((T, D))),
                 (bias_f[:, :], A["ffn_bias"][0:1, :].broadcast_to((T, D)))]
        WSPLIT = [(A["WkT"], WkH, WkL, c) for c in range(CC)] + [(A["WvT"], WvH, WvL, c) for c in range(CC)]

        def ring(t, b_par):
            return (t.i + 2 * b_par) % RING

        def before(b, t, n):
            if t.i >= n:
                return b, t.i - n
            return b.next(-1), ({0: 10, 1: 11, 2: 12, 3: 9}[t.i] if n == 4 else NT - n + t.i)

        def each_batch(eng, body):
            body(At(-1), 1, tiles=False, prev=False, nxt=True)
            body(At(0), 0, tiles=True, prev=False, nxt=True)
            with eng.Fori(0, (B - 2) // 2) as i:
                body(At(1, i, 2), 1, tiles=True, prev=True, nxt=True)
                body(At(2, i, 2), 0, tiles=True, prev=True, nxt=True)
            body(At(B - 1), 1, tiles=True, prev=True, nxt=False)
            body(At(B), 0, tiles=False, prev=True, nxt=False)

        def batch_of(dram, b, n):
            i = b.const + n if b.reg is None else b.reg * b.factor + (b.const + n)
            return dram[bass.ds(i, 1)].rearrange("o t d -> (o t) d")

        def tiles_at(s, b, par, tiles, prev, nxt):
            nb, np_ = b.next(1), 1 - par
            pb = b.next(-1)
            cur = [(b, par, t) for t in STEPS[s]] if tiles else []
            if s:
                last = [(b, par, t) for t in STEPS[s - 1]] if tiles else []
            else:
                last = [(pb, 1 - par, t) for t in STEPS[6]] if prev else []
            if s < 6:
                coming = [(b, par, t) for t in STEPS[s + 1]] if tiles else []
            else:
                coming = [(nb, np_, t) for t in STEPS[0]] if nxt else []
            return cur, last, coming

        def late_tile(s, b, par, tiles, prev):
            if s == 0:
                return [(b.next(-1), 1 - par, STEPS[5][1])] if prev else []
            return [(b, par, STEPS[s - 2][1])] if s > 1 and tiles else []

        def slices(s, part, b, par, tiles, nxt):
            if s == 0:
                return [(b, par, n) for n in PLAN[s][part]] if tiles else []
            return [(b.next(), 1 - par, n) for n in PLAN[s][part]] if nxt else []

        block = ctx.enter_context(nc.Block())

        @block.sync
        def _(sp):
            for t, a in SETUP:
                sp.dma_start(t, a).then_inc(setup_in, 16)
            for u, (w, _, _, c) in enumerate(WSPLIT):
                sp.dma_start(E[u % 4][:, 0:D] if u < 4 else S[u % 4][:, 0:D], w[128 * c:128 * c + 128, :]).then_inc(w_in, 16)

            def load_context(b, half):
                k0, kn = HALVES[half]
                i = b.const + 1 if b.reg is None else b.reg * b.factor + (b.const + 1)
                for piece in range(2):
                    need(sp, ctx_hi, b.next().count(4, 2 * half + piece))
                    need(sp, ctx_lo, b.next().count(4, 2 * half + piece))
                    src = A["ctxT"][bass.ds(i, 1), 256 * piece:256 * piece + 256, k0:k0 + kn]
                    sp.dma_start(raw[:, :, 0:kn], src.rearrange("o (c p) k -> p (o c) k", p=128)).then_inc(ctx_in, 16)

            def body(b, par, tiles, prev, nxt):
                if nxt:
                    load_context(b, 0)
                    need(sp, xn1_ready, b.count(1, 1))
                    need(sp, xb_ready, b.count(1, 1))
                    sp.dma_start(xin[:, :], batch_of(x1_dram, b, 1)).then_inc(x_in, 16)
                    load_context(b, 1)
                if prev:
                    sp.wait_ge(out_ready, b.count(1, 0))
                    sp.dma_start(batch_of(out_dram, b, -1), x2[:, :]).then_inc(x2_free, 16)
            sp.sem_inc(x2_free, 16)
            each_batch(sp, body)
            sp.wait_ge(x2_free, 16 * B + 16)

        @block.gpsimd
        def _(pool):
            for t in (QH[:, :, :], QL[:, :, :], RH[:, :], RL[:, :]):
                pool.memset(t.bitcast(F32), 0.0).then_inc(zeroed, 1)
            order = Order(pool, pool_order)
            order.mark(pool.memset(minus_half[:, :], -0.5))
            order.finish()

            def key_low(bn, pn, n):
                half, _, g = SLICES[n]
                k0, kn = HALVES[half]
                i = 4 * half + g
                pool.wait_ge(k_hi, bn.count(8, i + 1))
                pool.tensor_tensor(KL[pn][:, g, k0:k0 + kn], K32[:, 0:kn],
                                   KH[pn][:, g, k0:k0 + kn].bitcast(F32), ALU.subtract).then_inc(k_lo, 1)

            def context_low(bn, piece):
                kn, cs = HALVES[piece // 2][1], slice(2 * (piece % 2), 2 * (piece % 2) + 2)
                if piece % 2 == 0:
                    need(pool, kv_mm, bn.count(NSL, 7 * (piece // 2)))
                pool.wait_ge(ctx_hi, bn.count(4, piece + 1))
                pool.tensor_tensor(cL[:, cs, 0:kn], raw[:, :, 0:kn], cH[:, cs, 0:kn].bitcast(F32),
                                   ALU.subtract).then_inc(ctx_lo, 1)

            def body(b, par, tiles, prev, nxt):
                bn, pn = b.next(), 1 - par
                for s in range(7):
                    cur, last, coming = tiles_at(s, b, par, tiles, prev, nxt)
                    for tb, tp, t in last:
                        r = ring(t, tp)
                        pool.wait_ge(f_ready, tb.count(NT, t.i + 1))
                        pool.tensor_tensor(E[r][0:t.rows, :], E[r][0:t.rows, :], S[r][0:t.rows, :],
                                           ALU.subtract).then_inc(p_ready, 1)
                    if s == 2 and prev:
                        pool.wait_ge(var2_ready, b.count(1, 0))
                        pool.tensor_tensor(rstd[:, :], mv[:, 1:2], minus_half[:, :], ALU.pow).then_inc(rstd2_ready, 1)
                    if s == 3 and prev:
                        pool.wait_ge(xn2_ready, b.count(1, 0))
                        pool.tensor_tensor(x2[:, :], x2[:, :], bias_f[:, :], ALU.add).then_inc(x2f_ready, 1)
                    if s == 4 and nxt:
                        pool.wait_ge(var1_ready, bn.count(1, 1))
                        pool.tensor_tensor(rstd[:, :], mv[:, 1:2], minus_half[:, :], ALU.pow).then_inc(rstd1_ready, 1)
                        pool.wait_ge(bias_ready, 1)
                        pool.tensor_tensor(xb[pn][:, :], xin[:, :], bias_o[:, :], ALU.add).then_inc(xb_ready, 1)
                    if s in (0, 1, 3, 4) and nxt:
                        context_low(bn, 2 * (s // 3) + s % 3)
                    for x in slices(s, 0, b, par, tiles, nxt) + slices(s, 1, b, par, tiles, nxt):
                        if SLICES[x[2]][1] == "K":
                            key_low(*x)
                order.finish()
            each_batch(pool, body)

        @block.tensor
        def _(pe):
            pe.wait_ge(setup_in, 16 * len(SETUP))
            pe.wait_ge(zeroed, 5)
            for c in range(CC):
                last = pe.matmul(pX[0:T, :], xT[:, c, :], WoT[:, c, :], start=c == 0, stop=c == CC - 1)
            last.then_inc(bias_mm, 1)
            pe.wait_ge(bias_ready, 1)
            pe.wait_ge(w_lo, len(WSPLIT))

            def project(bn, pn, n):
                half, kind, k = SLICES[n]
                k0, kn = HALVES[half]
                if n % 7 == 0:
                    pe.wait_ge(ctx_lo, bn.count(4, 2 * half + 2))
                need(pe, kv_out, bn.count(NSL, n - 1))
                for c in range(CC):
                    if kind == "K":
                        cols = slice(128 * k, 128 * k + 128)
                        last = split3(pe, pF[:, n % 2, 0:kn], WkH[:, c, cols], WkL[:, c, cols],
                                      cH[:, c, 0:kn], cL[:, c, 0:kn], c == 0, c == CC - 1)
                    else:
                        keys = slice(KEY0[k] - k0, KEY0[k] - k0 + 128)
                        last = split3(pe, pF[:, n % 2, :], cH[:, c, keys], cL[:, c, keys],
                                      WvH[:, c, :], WvL[:, c, :], c == 0, c == CC - 1)
                last.then_inc(kv_mm, 1)

            def transposed(x, done):
                for c in range(CC):
                    last = pe.transpose(pX[:, T * c:T * c + T], x[:, 128 * c:128 * c + 128], ident[0:T, 0:T])
                last.then_inc(done, 1)

            def score(tb, tp, t):
                if t.i == 0:
                    pe.wait_ge(q_lo, tb.count(5, 5))
                if t.t == 0 or t.rest:
                    pe.wait_ge(k_lo, tb.count(8, 5 + min(t.g, 3)))
                need(pe, s_ready, tb.count(NT, t.i))
                parts = [(slice(0, 512 - SPLIT), slice(SPLIT, 512)), (slice(512 - SPLIT, KV), slice(512, KV + SPLIT))]
                for keys, cols in parts:
                    out = pS[0:t.rows, cols]
                    if t.rest:
                        for g in range(4):
                            rows = slice(t.rows * g, t.rows * g + t.rows)
                            last = split3(pe, out, RH[:, rows], RL[:, rows], KH[tp][:, g, keys], KL[tp][:, g, keys],
                                          g == 0, g == 3)
                    else:
                        rows = slice(128 * t.t, 128 * t.t + 128)
                        last = split3(pe, out, QH[:, t.g, rows], QL[:, t.g, rows],
                                      KH[tp][:, t.g, keys], KL[tp][:, t.g, keys], True, True)
                last.then_inc(s_mm, 1)

            def weights_T(tb, tp, t):
                pe.wait_ge(p_ready, tb.count(NT, t.i + 1))
                need(pe, pt_ready, tb.count(NT, t.i))
                settle(pe)
                for k in range(KC):
                    last = pe.transpose(pT[:, 128 * k:128 * k + t.rows],
                                        E[ring(t, tp)][0:t.rows, KEY0[k]:KEY0[k] + 128], ident[0:t.rows, 0:t.rows])
                last.then_inc(pt_mm, 1)

            def values(tb, tp, t):
                pe.wait_ge(pt_ready, tb.count(NT, t.i + 1))
                need(pe, ot_ready, tb.count(NT, t.i))
                if t.i == 0:
                    pe.wait_ge(kv_out, tb.count(NSL, NSL))
                for k in range(KC):
                    if t.rest:
                        rhs = V[tp][:, k, :].rearrange("p (g h d) -> p g h d", g=4, h=4)[:, :, 3, :]
                    else:
                        h = 4 * t.g + t.t
                        rhs = V[tp][:, k, DH * h:DH * h + t.dims]
                    out = pO[0:t.rows, 0:t.dims]
                    if t.rest:
                        out = out.rearrange("p (g d) -> p g d", g=4)
                    last = pe.matmul(out, PT[:, k, 0:t.rows], rhs, start=k == 0, stop=k == KC - 1)
                last.then_inc(o_mm, 1)

            def output_T(tb, tp, t):
                pe.wait_ge(o_ready, tb.count(NT, t.i + 1))
                settle(pe)
                pe.transpose(pO[0:t.dims, 256:256 + t.rows], On[0:t.rows, 0:t.dims],
                             ident[0:t.rows, 0:t.rows]).then_inc(ot_mm, 1)

            def body(b, par, tiles, prev, nxt):
                bn = b.next()
                for s in range(7):
                    cur, last, coming = tiles_at(s, b, par, tiles, prev, nxt)
                    if s == 1 and prev:
                        pe.wait_ge(ot_ready, b.count(NT, 0))
                        for c in range(CC):
                            ins = pe.matmul(pX[0:T, :], ctxT[:, c, :], WoT[:, c, :], start=c == 0, stop=c == CC - 1)
                        ins.then_inc(y_mm, 1)
                    if s == 3 and prev:
                        pe.wait_ge(xn2_ready, b.count(1, 0))
                        transposed(xn, x2T_mm)
                    if s == 4 and prev:
                        pe.wait_ge(x2T_ready, b.count(1, 0))
                        for c in range(CC):
                            ins = pe.matmul(pX[0:T, :], xT[:, c, :], M[:, c, :], start=c == 0, stop=c == CC - 1)
                        ins.then_inc(f_mm, 1)
                    if coming and s < 6:
                        score(*coming[0])
                    for x in late_tile(s, b, par, tiles, prev):
                        values(*x)
                    for x in slices(s, 0, b, par, tiles, nxt):
                        project(*x)
                    if last:
                        weights_T(*last[0])
                    for x in late_tile(s, b, par, tiles, prev):
                        output_T(*x)
                    if s < 6 and len(coming) > 1:
                        score(*coming[1])
                    if s == 5 and nxt:
                        need(pe, out_ready, b.count(1, 0))
                        pe.wait_ge(xn1_ready, bn.count(1, 1))
                        transposed(xn, x1T_mm)
                    if last:
                        values(*last[0])
                    if s == 6 and coming:
                        score(*coming[0])
                    if len(last) > 1:
                        weights_T(*last[1])
                    if s == 6 and coming:
                        score(*coming[1])
                    if s == 5 and last:
                        output_T(*last[0])
                    for x in slices(s, 1, b, par, tiles, nxt):
                        project(*x)
                    if s == 5 and nxt:
                        pe.wait_ge(x1T_ready, bn.count(1, 1))
                        for o in range(CC):
                            for c in range(CC):
                                ins = pe.matmul(pX[:, T * o:T * o + T], WqT[:, c, 128 * o:128 * o + 128], xT[:, c, :],
                                                start=c == 0, stop=c == CC - 1)
                        ins.then_inc(q_mm, 1)
                    if s != 5 and last:
                        output_T(*last[0])
            each_batch(pe, body)

        @block.scalar
        def _(act):
            for u, (_, wh, _, c) in enumerate(WSPLIT):
                src = E[u % 4] if u < 4 else S[u % 4]
                act.wait_ge(w_in, 16 * len(WSPLIT))
                act.activation(wh[:, c, :], src[:, 0:D], ACT.Copy).then_inc(w_hi, 1)
            act.wait_ge(setup_in, 16 * len(SETUP))
            act.wait_ge(w_lo, len(WSPLIT))
            act.wait_ge(zeroed, 5)

            def context_high(bn, piece):
                kn, cs = HALVES[piece // 2][1], slice(2 * (piece % 2), 2 * (piece % 2) + 2)
                if piece % 2 == 0:
                    need(act, kv_mm, bn.count(NSL, 7 * (piece // 2)))
                act.wait_ge(ctx_in, bn.count(64, 16 * (piece + 1)))
                act.activation(cH[:, cs, 0:kn], raw[:, :, 0:kn], ACT.Copy).then_inc(ctx_hi, 1)

            def keep(bn, pn, n):
                half, kind, k = SLICES[n]
                act.wait_ge(kv_mm, bn.count(NSL, n + 1))
                if kind == "V":
                    scale = tail_keys[:, 0:1] if k == KC - 1 else 1.0
                    act.activation(V[pn][:, k, :], pF[:, n % 2, :], ACT.Copy, scale=scale).then_inc(kv_out, 1)
                    return
                k0, kn = HALVES[half]
                i = 4 * half + k
                need(act, k_lo, bn.count(8, i))
                act.activation(K32[:, 0:kn], pF[:, n % 2, 0:kn], ACT.Identity,
                               bias=bk[:, k:k + 1]).then_inc(kv_out, 1)
                act.wait_ge(kv_out, bn.count(NSL, n + 1))
                act.activation(KH[pn][:, k, k0:k0 + kn], K32[:, 0:kn], ACT.Copy).then_inc(k_hi, 1)

            def exps_left(tb, tp, t):
                r, rows = ring(t, tp), slice(0, t.rows)
                act.wait_ge(picked, tb.count(NT, t.i + 1))
                act.wait_ge(e_ready, tb.count(NT, t.i + 1))
                act.activation(S[r][rows, :], W[(t.i + tp) % 2][rows, :], ACT.Exp, bias=shift[rows, r:r + 1],
                               scale=SCALE).then_inc(f_ready, 1)
                act.activation(top[r][rows, :], top[r][rows, :], ACT.Exp, bias=shift[rows, r:r + 1],
                               scale=SCALE, accum_out=Z[rows, r:r + 1]).then_inc(z_ready, 1)

            def exps(tb, tp, t):
                r, rows = ring(t, tp), slice(0, t.rows)
                ob, oi = before(tb, t, RING)
                need(act, pt_mm, ob.count(NT, oi + 1))
                act.wait_ge(shift_ready, tb.count(NT, t.i + 1))
                act.activation(E[r][rows, :], S[r][rows, :], ACT.Exp, bias=shift[rows, r:r + 1],
                               scale=SCALE).then_inc(e_ready, 1)

            def keep_scores(tb, tp, t):
                ob, oi = before(tb, t, RING)
                need(act, p_ready, ob.count(NT, oi + 1))
                act.wait_ge(s_mm, tb.count(NT, t.i + 1))
                act.activation(S[ring(t, tp)][0:t.rows, :], scores[0:t.rows, :], ACT.Copy).then_inc(s_ready, 1)

            def keep_weights_T(tb, tp, t):
                need(act, o_mm, tb.count(NT, t.i))
                act.wait_ge(pt_mm, tb.count(NT, t.i + 1))
                act.activation(PT[:, :, 0:t.rows], chunks(pT[:, 0:KC * 128], KC)[:, :, 0:t.rows],
                               ACT.Copy).then_inc(pt_ready, 1)

            def normalise(tb, tp, t):
                r = ring(t, tp)
                act.wait_ge(rz_ready, tb.count(NT, t.i + 1))
                act.wait_ge(o_mm, tb.count(NT, t.i + 1))
                need(act, ot_mm, tb.count(NT, t.i))
                act.activation(On[0:t.rows, 0:t.dims], pO[0:t.rows, 0:t.dims], ACT.Copy,
                               scale=rZ[0:t.rows, r:r + 1]).then_inc(o_ready, 1)

            def place_output(tb, tp, t):
                if t.i == 0:
                    need(act, y_mm, tb.count(1, 0))
                act.wait_ge(ot_mm, tb.count(NT, t.i + 1))
                for p, cols, to, g, q in t.blocks():
                    ins = act.activation(ctxT[to:to + DH, g, q], pO[p:p + DH, 256 + cols.start:256 + cols.stop], ACT.Copy)
                ins.then_inc(ot_ready, 1)

            def body(b, par, tiles, prev, nxt):
                bn, pn = b.next(), 1 - par
                for s in range(7):
                    cur, last, coming = tiles_at(s, b, par, tiles, prev, nxt)
                    for x in last:
                        exps_left(*x)
                    if s == 6 and nxt:
                        act.wait_ge(q_mm, bn.count(1, 1))
                        for c in range(CC):
                            act.activation(xT[:, c, :], pX[:, T * c:T * c + T], ACT.Identity,
                                           bias=bq[:, c:c + 1]).then_inc(q_ready, 1)
                        need(act, s_mm, b.count(NT, NT))
                        act.wait_ge(q_ready, bn.count(CC, CC))
                        for h in range(4):
                            rows = slice(DH * h, DH * h + DH)
                            act.activation(QH[rows, :, T * h:T * h + T], xT[rows, :, :], ACT.Copy).then_inc(q_hi, 1)
                        act.activation(chunks(RH[3 * DH:128, :], 4)[:, :, 0:REST], xT[3 * DH:128, :, T - REST:T],
                                       ACT.Copy).then_inc(q_hi, 1)
                    for x in cur:
                        exps(*x)
                    if s == 3 and prev:
                        act.wait_ge(x2T_mm, b.count(1, 0))
                        act.activation(xT[:, :, :], chunks(pX[:, 0:CC * T], CC), ACT.Copy).then_inc(x2T_ready, 1)
                    if s in (1, 4) and nxt:
                        context_high(bn, 2 * (s // 3) + 1)
                    if coming and s < 6:
                        keep_scores(*coming[0])
                    for x in late_tile(s, b, par, tiles, prev):
                        normalise(*x)
                    for x in slices(s, 0, b, par, tiles, nxt):
                        keep(*x)
                    if last:
                        keep_weights_T(*last[0])
                    for x in late_tile(s, b, par, tiles, prev):
                        place_output(*x)
                    if s == 0 and nxt:
                        context_high(bn, 0)
                    if s < 6 and len(coming) > 1:
                        keep_scores(*coming[1])
                    if s == 5 and nxt:
                        act.wait_ge(x1T_mm, bn.count(1, 1))
                        act.activation(xT[:, :, :], chunks(pX[:, 0:CC * T], CC), ACT.Copy).then_inc(x1T_ready, 1)
                    if last:
                        normalise(*last[0])
                    if s == 6 and coming:
                        keep_scores(*coming[0])
                    if len(last) > 1:
                        keep_weights_T(*last[1])
                    if s == 6 and coming:
                        keep_scores(*coming[1])
                    if s == 5 and last:
                        place_output(*last[0])
                    for x in slices(s, 1, b, par, tiles, nxt):
                        keep(*x)
                    if s != 5 and last:
                        place_output(*last[0])
                    if s == 3 and nxt:
                        context_high(bn, 2)
            each_batch(act, body)

        @block.vector
        def _(dve):
            order = Order(dve, dve_order)
            dve.wait_ge(setup_in, 16 * len(SETUP))
            dve.tensor_copy(xT[:, :, :], bv[:, :].unsqueeze(2).broadcast_to((128, CC, T))).then_inc(zeroed, 1)
            for u, (_, wh, wl, c) in enumerate(WSPLIT):
                src = E[u % 4] if u < 4 else S[u % 4]
                dve.wait_ge(w_hi, u + 1)
                dve.tensor_tensor(wl[:, c, :], src[:, 0:D], wh[:, c, :].bitcast(F32), ALU.subtract).then_inc(w_lo, 1)
            dve.wait_ge(bias_mm, 1)
            dve.tensor_tensor(bias_o[:, :], pX[0:T, :], bias_o[:, :], ALU.add).then_inc(bias_ready, 1)

            def body(b, par, tiles, prev, nxt):
                bn = b.next()
                for s in range(7):
                    cur, last, coming = tiles_at(s, b, par, tiles, prev, nxt)
                    step_of = {}
                    for tb, tp, t in cur:
                        r, rows = ring(t, tp), slice(0, t.rows)
                        ob, oi = before(tb, t, RING)
                        need(dve, z_ready, ob.count(NT, oi + 1))
                        dve.wait_ge(s_ready, tb.count(NT, t.i + 1))
                        settle(dve)
                        order.after(max(order.n - 2, 0))
                        step_of[t.i] = order.mark(dve.max(top[r][rows, 0:8], S[r][rows, :]))
                    for tb, tp, t in cur:
                        r, rows = ring(t, tp), slice(0, t.rows)
                        order.after(step_of[t.i])
                        dve.tensor_scalar(shift[rows, r:r + 1], top[r][rows, 0:1], -SCALE, None,
                                          ALU.mult).then_inc(shift_ready, 1)
                    for k in range(TOPK // 8):
                        for tb, tp, t in cur:
                            r, rows, w = ring(t, tp), slice(0, t.rows), W[(t.i + tp) % 2]
                            eight = top[r][rows, 8 * k:8 * k + 8]
                            if k:
                                order.after(step_of[t.i])
                                step_of[t.i] = order.mark(dve.max(eight, w[rows, :]))
                        for tb, tp, t in cur:
                            r, rows, w = ring(t, tp), slice(0, t.rows), W[(t.i + tp) % 2]
                            eight = top[r][rows, 8 * k:8 * k + 8]
                            if k == 0:
                                ob, oi = before(tb, t, 2)
                                need(dve, f_ready, ob.count(NT, oi + 1))
                                settle(dve)
                            order.after(step_of[t.i])
                            ins = dve.match_replace(w[rows, :], eight, (w if k else S[r])[rows, :], REMOVED)
                            if k == TOPK // 8 - 1:
                                ins.then_inc(picked, 1)
                            else:
                                step_of[t.i] = order.mark(ins)
                        if k == 0:
                            for tb, tp, t in last:
                                r, rows = ring(t, tp), slice(0, t.rows)
                                dve.wait_ge(z_ready, tb.count(NT, t.i + 1))
                                dve.reciprocal(rZ[rows, r:r + 1], Z[rows, r:r + 1]).then_inc(rz_ready, 1)
                            if s == 2 and prev:
                                row_stats(dve, order, x2[:, :], stats[:, :], mv[:, :], var2_ready)
                            if s == 4 and nxt:
                                dve.wait_ge(x_in, bn.count(16, 16))
                                row_stats(dve, order, xin[:, :], stats[:, :], mv[:, :], var1_ready)
                        if k == 1 and s == 4 and prev:
                            dve.wait_ge(f_mm, b.count(1, 0))
                            dve.wait_ge(x2f_ready, b.count(1, 0))
                            dve.tensor_tensor(x2[:, :], pX[0:T, :], x2[:, :], ALU.add).then_inc(out_ready, 1)
                        if k == 1 and s == 6 and nxt:
                            for h in range(4):
                                rows, cols = slice(DH * h, DH * h + DH), slice(T * h, T * h + T)
                                dve.wait_ge(q_hi, bn.count(5, h + 1))
                                dve.tensor_tensor(QL[rows, :, cols], xT[rows, :, :], QH[rows, :, cols].bitcast(F32),
                                                  ALU.subtract).then_inc(q_lo, 1)
                            dve.wait_ge(q_hi, bn.count(5, 5))
                            dve.tensor_tensor(chunks(RL[3 * DH:128, :], 4)[:, :, 0:REST], xT[3 * DH:128, :, T - REST:T],
                                              chunks(RH[3 * DH:128, :], 4)[:, :, 0:REST].bitcast(F32),
                                              ALU.subtract).then_inc(q_lo, 1)
                        if k == 2 and s == 1 and prev:
                            dve.wait_ge(y_mm, b.count(1, 0))
                            dve.wait_ge(xb_ready, b.count(1, 0))
                            dve.wait_ge(x2_free, b.count(16, 0))
                            dve.tensor_tensor(x2[:, :], pX[0:T, :], xb[1 - par][:, :], ALU.add).then_inc(x2_ready, 1)
                            dve.wait_ge(x2_ready, b.count(1, 0))
                            settle(dve)
                        if k == 2 and s == 2 and prev:
                            need(dve, x1T_mm, b.count(1, 1) if nxt or tiles else b.count(1, 0))
                            dve.wait_ge(rstd2_ready, b.count(1, 0))
                            dve.tensor_scalar(xn[:, :], x2[:, :], mv[:, 0:1], rstd[:, :],
                                              ALU.subtract, ALU.mult).then_inc(xn2_ready, 1)
                        if k == 2 and s == 4 and nxt:
                            need(dve, x2T_mm, b.count(1, 0))
                            dve.wait_ge(rstd1_ready, bn.count(1, 1))
                            dve.tensor_scalar(xn[:, :], xin[:, :], mv[:, 0:1], rstd[:, :],
                                              ALU.subtract, ALU.mult).then_inc(xn1_ready, 1)
                order.finish()
            each_batch(dve, body)


def program(nc, A, out):
    x1_dram = nc.dram_tensor("x1_scratch", (B, T, D), F32, kind="Internal").ap()
    self_program(nc, A, x1_dram)
    with nc.sbuf_tensor("spectral_M", [128, CC, D], F32) as M:
        spectral_program(nc, A, M)
        cross_program(nc, A, M, x1_dram, out)


def kernel(**inputs):
    import concourse.bacc as bacc
    from concourse.bass_utils import run_bass_kernel_spmd

    a = {k: np.asarray(v) for k, v in inputs.items()}
    row = lambda v: np.ascontiguousarray(v).reshape(1, -1)
    cols = lambda v: np.ascontiguousarray(v.reshape(-1, 128).T)
    swap = lambda v: np.ascontiguousarray(np.swapaxes(v, -1, -2))
    f32 = lambda v: np.ascontiguousarray(v.astype(np.float32))
    n = np.arange(D)
    k = np.where(n <= D // 2, n, n - D // 2)
    sine = n > D // 2
    angle = 2.0 * np.pi * (np.outer(k, n) % D) / D
    dft = np.where(sine[:, None], np.sin(angle), np.cos(angle))
    single = (k == 0) | (k == D // 2)
    even_m = np.array([[1, 1], [1, -1], [1, 1], [1, -1]])
    odd_m = np.array([[-1, 1], [-1, -1], [1, -1], [1, 1]])
    signs = np.where(sine[:, None, None], odd_m, even_m) * np.where(single[:, None], [1, 1, 0, 0], 1)[:, :, None]
    wr, wi = a["L0_ffn_w_freq_real"], a["L0_ffn_w_freq_imag"]
    same = sine[:, None] == sine[None, :]
    fold = lambda ks, ms: np.ascontiguousarray(
        np.where(same, wr[np.ix_(ks * k % D, ms * k % D)], wi[np.ix_(ks * k % D, ms * k % D)]).T)
    freq = 1.0 / 10000.0 ** (np.arange(0, DH, 2) / DH)
    rope = np.arange(T)[:, None] * freq[None, :]
    arrays = {
        "cos": f32(np.cos(rope)), "sin": f32(np.sin(rope)), "ident": np.eye(128, dtype=np.float32),
        "dft": f32(dft),
        "fold_signs": f32(signs.reshape(CC, 128, 4, 2).transpose(1, 0, 2, 3)),
        "tail_keys": f32((np.arange(128) >= 6 * 128 - KV).reshape(128, 1)),
        "x": a["x"], "ctxT": swap(a["ctx_1024"]),
        "WQ": a["L0_attn_WQ"], "bQ": row(a["L0_attn_bQ"]), "WK": a["L0_attn_WK"], "bK": row(a["L0_attn_bK"]),
        "WV": a["L0_attn_WV"], "bV": row(a["L0_attn_bV"]), "WO": a["L0_attn_WO"], "bO": row(a["L0_attn_bO"]),
        "sinks": row(a["L0_attn_sink_scalars"]), "v_nulls": row(a["L0_attn_v_nulls"]),
        "bV_cols": cols(a["L0_attn_bV"]), "v_nulls_cols": cols(a["L0_attn_v_nulls"]),
        "sinks_cols": cols(np.repeat(a["L0_attn_sink_scalars"], DH)),
        "WqT": swap(a["L0_xattn_Wq"]), "WkT": swap(a["L0_xattn_Wk"]),
        "WvT": swap(a["L0_xattn_Wv"]), "WoT": swap(a["L0_xattn_Wo"]),
        "xbq": cols(a["L0_xattn_bq"]), "xbk": cols(a["L0_xattn_bk"]),
        "xbv": cols(a["L0_xattn_bv"]), "xbo": row(a["L0_xattn_bo"]),
        "Wpp": fold(1, 1), "Wmp": fold(-1, 1), "Wpm": fold(1, -1), "Wmm": fold(-1, -1),
        "ffn_bias": row(a["L0_ffn_bias"]),
    }
    nc = bacc.Bacc("TRN2", target_bir_lowering=False, num_devices=1)
    A = {k: nc.dram_tensor("in_" + k, v.shape, F32, kind="ExternalInput").ap() for k, v in arrays.items()}
    out = nc.dram_tensor("out", (B, T, D), F32, kind="ExternalOutput").ap()
    program(nc, A, out)
    r = run_bass_kernel_spmd(nc, [{"in_" + k: v for k, v in arrays.items()}], core_ids=[0])
    return r.results[0]["out"]
```
